# Optimizing a Trainium2 kernel written in Bass

```python
import numpy as np
import jax
import jax.numpy as jnp

def _softmax(x, axis=-1):
    return jax.nn.softmax(x, axis=axis)

def _gelu(x):
    return jax.nn.gelu(x, approximate=True)

def _silu(x):
    return jax.nn.silu(x)

def _sigmoid(x):
    return jax.nn.sigmoid(x)

def _layernorm(x, axis=-1, eps=1e-05):
    m = jnp.mean(x, axis=axis, keepdims=True)
    v = jnp.var(x, axis=axis, keepdims=True)
    return (x - m) / jnp.sqrt(v + eps)

def _scatter_add(tgt, idx, src, axis=0):
    return tgt.at[idx].add(src)

def _segment_sum(src, seg, n):
    return jax.ops.segment_sum(src, seg, n)
kernel_name = 'mk_xattn_ffn_d1_seqx_r8_feebc7'

def setup_inputs(seed: int=0):
    np.random.seed(seed)
    _w = jnp.asarray

    def _rec_inputs():
        import jax
        import jax.numpy as jnp
        _rk = jax.random.key(seed)
        x = 7.22e-05 + 1 * jax.random.normal(jax.random.fold_in(_rk, 1), (64, 128, 128), jnp.float32)
        _lenS = 128 - jax.random.randint(jax.random.fold_in(_rk, 7), (64,), 0, max(1, 128 // 4) + 1, jnp.int32)
        _lenS2 = 77 - jax.random.randint(jax.random.fold_in(_rk, 8), (64,), 0, max(1, 77 // 4) + 1, jnp.int32)
        _ctx_768P = jax.random.normal(jax.random.fold_in(_rk, 11), (64, 16, 96), jnp.float32)
        _ctx_768c = jax.random.dirichlet(jax.random.fold_in(_rk, 511), 0.3 * jnp.ones((16,), jnp.float32), (64, 77))
        _ctx_768t = jnp.einsum('bsk,bkd->bsd', _ctx_768c, _ctx_768P)
        _ctx_768t = _ctx_768t * jax.lax.rsqrt(jnp.mean(jnp.square(_ctx_768t)) + 1e-12) * 0.953939
        ctx_768 = -7.36909e-05 + 0.999899 * (_ctx_768t + 0.3 * jax.random.normal(jax.random.fold_in(_rk, 611), (64, 77, 96), jnp.float32))
        return (x, ctx_768)
    x, ctx_768 = _rec_inputs()

    def _L0_xattn_setup():
        import jax, jax.numpy as jnp
        import numpy as np
        NUM_HEADS = 16
        HEAD_DIM = 64
        INNER = NUM_HEADS * HEAD_DIM
        QUERY_DIM = 128
        CONTEXT_DIM = 96
        SCALE = HEAD_DIM ** (-0.5)
        key = jax.random.key(seed)
        ks = jax.random.split(key, 6)
        B, NQ, NKV = (8, 128, 256)
        query = jax.random.normal(ks[0], (B, NQ, QUERY_DIM), dtype=jnp.float32)
        context = jax.random.normal(ks[1], (B, NKV, CONTEXT_DIM), dtype=jnp.float32)
        w_q = jax.random.normal(ks[2], (QUERY_DIM, INNER), dtype=jnp.float32) * QUERY_DIM ** (-0.5)
        w_kv = jax.random.normal(ks[3], (CONTEXT_DIM, 2 * INNER), dtype=jnp.float32) * CONTEXT_DIM ** (-0.5)
        w_out = jax.random.normal(ks[4], (INNER, QUERY_DIM), dtype=jnp.float32) * INNER ** (-0.5)
        b_out = jax.random.normal(ks[5], (QUERY_DIM,), dtype=jnp.float32) * 0.01
        return {'query': query, 'context': context, 'w_q': w_q, 'w_kv': w_kv, 'w_out': w_out, 'b_out': b_out}
    _L0_xattn_all = _L0_xattn_setup()
    _L0_xattn_in = {k: v for k, v in _L0_xattn_all.items() if k in ('w_q', 'w_kv', 'w_out', 'b_out')}
    del _L0_xattn_all

    def _L0_ffn_setup():
        import jax, jax.numpy as jnp
        import numpy as np
        H = 128
        I = 176
        E = 8
        TOPK = 2
        ROUTING_SCALE = 1.0
        W_STD = 0.02
        key = jax.random.key(seed)
        ks = jax.random.split(key, 8)
        x = jax.random.normal(ks[0], (2, 128, H), dtype=jnp.float32)
        router_w = jax.random.normal(ks[1], (E, H), dtype=jnp.float32) * W_STD
        w1 = jax.random.normal(ks[2], (E, I, H), dtype=jnp.float32) * W_STD
        w2 = jax.random.normal(ks[3], (E, H, I), dtype=jnp.float32) * W_STD
        w3 = jax.random.normal(ks[4], (E, I, H), dtype=jnp.float32) * W_STD
        sw1 = jax.random.normal(ks[5], (I, H), dtype=jnp.float32) * W_STD
        sw2 = jax.random.normal(ks[6], (H, I), dtype=jnp.float32) * W_STD
        sw3 = jax.random.normal(ks[7], (I, H), dtype=jnp.float32) * W_STD
        return {'x': x, 'router_w': router_w, 'w1': w1, 'w2': w2, 'w3': w3, 'sw1': sw1, 'sw2': sw2, 'sw3': sw3}
    _L0_ffn_all = _L0_ffn_setup()
    _L0_ffn_in = {k: v for k, v in _L0_ffn_all.items() if k in ('router_w', 'w1', 'w2', 'w3', 'sw1', 'sw2', 'sw3')}
    del _L0_ffn_all
    return {'x': x, 'ctx_768': ctx_768, 'L0_xattn_w_q': _L0_xattn_in['w_q'], 'L0_xattn_w_kv': _L0_xattn_in['w_kv'], 'L0_xattn_w_out': _L0_xattn_in['w_out'], 'L0_xattn_b_out': _L0_xattn_in['b_out'], 'L0_ffn_router_w': _L0_ffn_in['router_w'], 'L0_ffn_w1': _L0_ffn_in['w1'], 'L0_ffn_w2': _L0_ffn_in['w2'], 'L0_ffn_w3': _L0_ffn_in['w3'], 'L0_ffn_sw1': _L0_ffn_in['sw1'], 'L0_ffn_sw2': _L0_ffn_in['sw2'], 'L0_ffn_sw3': _L0_ffn_in['sw3']}

def reference(x, ctx_768, L0_xattn_w_q, L0_xattn_w_kv, L0_xattn_w_out, L0_xattn_b_out, L0_ffn_router_w, L0_ffn_w1, L0_ffn_w2, L0_ffn_w3, L0_ffn_sw1, L0_ffn_sw2, L0_ffn_sw3):
    import jax
    import jax.numpy as jnp

    def _L0_xattn_ref(query, context, w_q, w_kv, w_out, b_out):
        import jax, jax.numpy as jnp
        import numpy as np
        NUM_HEADS = 16
        HEAD_DIM = 64
        INNER = NUM_HEADS * HEAD_DIM
        QUERY_DIM = 128
        CONTEXT_DIM = 96
        SCALE = HEAD_DIM ** (-0.5)
        B, NQ, _ = query.shape
        NKV = context.shape[1]
        q = query @ w_q
        kv = context @ w_kv
        k, v = jnp.split(kv, 2, axis=-1)
        q = q.reshape(B, NQ, NUM_HEADS, HEAD_DIM).transpose(0, 2, 1, 3)
        k = k.reshape(B, NKV, NUM_HEADS, HEAD_DIM).transpose(0, 2, 1, 3)
        v = v.reshape(B, NKV, NUM_HEADS, HEAD_DIM).transpose(0, 2, 1, 3)
        scores = jnp.einsum('bhqd,bhkd->bhqk', q, k) * SCALE
        attn = jax.nn.softmax(scores, axis=-1)
        out = jnp.einsum('bhqk,bhkd->bhqd', attn, v)
        out = out.transpose(0, 2, 1, 3).reshape(B, NQ, INNER)
        return out @ w_out + b_out

    def _L0_ffn_ref(x, router_w, w1, w2, w3, sw1, sw2, sw3):
        import jax, jax.numpy as jnp
        import numpy as np
        H = 128
        I = 176
        E = 8
        TOPK = 2
        ROUTING_SCALE = 1.0
        W_STD = 0.02
        B, S, _ = x.shape
        x2 = x.reshape(-1, H)
        T = x2.shape[0]
        logits = x2 @ router_w.T
        scores = jax.nn.softmax(logits, axis=-1)
        _, idx = jax.lax.top_k(scores, TOPK)
        rw = jax.lax.stop_gradient(jnp.take_along_axis(logits, idx, axis=-1))
        rw = rw * ROUTING_SCALE
        gate = jnp.zeros((T, E), dtype=x2.dtype)
        gate = gate.at[jnp.arange(T)[:, None], idx].add(rw)
        moe_out = jnp.zeros_like(x2)
        for e in range(E):
            h = jax.nn.silu(x2 @ w1[e].T) * (x2 @ w3[e].T)
            y = h @ w2[e].T
            moe_out = moe_out + gate[:, e:e + 1] * y
        sh = jax.nn.silu(x2 @ sw1.T) * (x2 @ sw3.T)
        moe_out = moe_out + sh @ sw2.T
        return moe_out.reshape(B, S, H)
    x = x + _L0_xattn_ref(_layernorm(x, axis=-1), ctx_768, L0_xattn_w_q, L0_xattn_w_kv, L0_xattn_w_out, L0_xattn_b_out)
    x = x + _L0_ffn_ref(_layernorm(x, axis=-1), L0_ffn_router_w, L0_ffn_w1, L0_ffn_w2, L0_ffn_w3, L0_ffn_sw1, L0_ffn_sw2, L0_ffn_sw3)
    return x

_drawn_inputs = setup_inputs


def setup_inputs(seed=0):
    import zlib

    import numpy as np

    out = dict(_drawn_inputs(seed))
    spreads = {}
    factors = {'L0_xattn_b_out': 5.546,
     'L0_ffn_router_w': 8.0,
     'L0_ffn_w1': 8.0,
     'L0_ffn_w2': 8.0,
     'L0_ffn_w3': 8.0,
     'L0_ffn_sw1': 8.0,
     'L0_ffn_sw2': 8.0,
     'L0_ffn_sw3': 8.0}
    for name, (base, spread) in spreads.items():
        noise = np.random.default_rng([zlib.crc32(name.encode()), seed]).standard_normal(out[name].shape)
        drawn = base * np.exp(spread * noise) if base else spread * noise
        out[name] = jnp.asarray(drawn.astype(out[name].dtype))
    for name, factor in factors.items():
        out[name] = (out[name] * factor).astype(out[name].dtype)
    return out
```

```python
import numpy as np
import concourse.bass as bass
from concourse import mybir
from contextlib import ExitStack

NB, NQ, D = 64, 128, 128
NK, DC = 77, 96
H, DH = 16, 64
E, I, TOPK = 8, 176, 2
GB = 4
NG = NB // GB
HK = H * NK
KR = 96
FU = (E + 1) * I
FC = -(-FU // 128)
FP = FC * 128
SP = [(0, 6), (6, 12), (12, 16)]
OP = [(0, 6), (6, 11), (11, 16)]
GR = 16
EPS = 1e-5
VBOOST = 128.0
TINY = 2.0 ** -60
BIG = 3.0e38


def program(nc, x_d, ctx_d, ctxflat_d, wq_d, wk_d, wv_d, wo_d, bo_d, rw_d, w1_d, w3_d, w2_d, sel_d,
            ident_d, rank_d, out_d):
    F, R, HF, BF, U = (mybir.dt.float32, mybir.dt.float32r, mybir.dt.float16, mybir.dt.bfloat16,
                       mybir.dt.uint32)
    ACT, ALU, AX = mybir.ActivationFunctionType, mybir.AluOpType, mybir.AxisListType
    ds = bass.ds
    stack = ExitStack()
    with stack:
        def sb(name, shape, dt=F):
            return stack.enter_context(nc.sbuf_tensor(name, shape, dt))

        def bank(name):
            return stack.enter_context(nc.psum_tensor(name, [128, 512], F))

        def sem(name):
            return stack.enter_context(nc.semaphore(name))

        X = sb("X", [128, NB, D])
        ctx_raw = sb("ctx_raw", [DC, NB * NK])
        a_hi = sb("a_hi", [128, H * D], R)
        a_lo = sb("a_lo", [128, H * D], R)
        wv_hi = sb("wv_hi", [DC, H * DH], R)
        wv_lo = sb("wv_lo", [DC, H * DH], R)
        wo = sb("wo", [128, 8, D])
        G = sb("G", [128, 2 * GB, H, NK])
        cg_hi = sb("cg_hi", [DC, GB * NK], R)
        cg_lo = sb("cg_lo", [DC, GB * NK], R)
        cv_hi = sb("cv_hi", [DC, 2, NK], R)
        cv_lo = sb("cv_lo", [DC, 2, NK], R)
        xln = sb("xln", [128, 2, D])
        xT = sb("xT", [128, 2, NQ])
        P = sb("P", [128, 2, HK])
        pt_hi = sb("pt_hi", [128, 2, H * NQ], HF)
        pt_lo = sb("pt_lo", [128, 2, H * NQ], HF)
        v_hi = sb("v_hi", [KR, 2, H, DH + 1], HF)
        v_lo = sb("v_lo", [KR, 2, H, DH + 1], HF)
        O = sb("O", [128, 2, H * DH])
        OT = sb("OT", [128, 2, 8, NQ])
        xb = sb("xb", [128, 2, D])
        bo = sb("bo", [128, D])
        top = sb("top", [128, 2, H])
        rec = sb("rec", [128, 2, H])
        bn = sb("bn", [128, 6])
        mv = sb("mv", [128, 2, 2])
        ve = sb("ve", [128, 4])
        rstd = sb("rstd", [128, 2])
        half = sb("half", [128, 4])
        ident = sb("ident", [128, 128])
        w1_hi = sb("w1_hi", [128, FP], R)
        w1_lo = sb("w1_lo", [128, FP], R)
        w3_hi = sb("w3_hi", [128, FP], R)
        w3_lo = sb("w3_lo", [128, FP], R)
        rw = sb("rw", [128, E])
        rw_hi = sb("rw_hi", [128, E], R)
        rw_lo = sb("rw_lo", [128, E], R)
        sel = sb("sel", [128, FP], BF)
        amax = sb("amax", [128, 2])
        amall = sb("amall", [128, 2])
        sc = sb("sc", [128, 8])
        rank = sb("rank", [128, GB, E])

        wq_raw = O[0:DH, :, :].rearrange("p a n -> p (a n)")
        wk_raw = OT[0:DH, :, :, :].rearrange("p a c n -> p (a c n)")
        P_flat = P[:, :, :].rearrange("p a n -> p (a n)")
        wv_raw, wo_raw = P_flat[0:DC, 0:H * DH], P_flat[:, H * DH:2 * H * DH]
        w1_raw = pt_hi[:, :, :].rearrange("p a n -> p (a n)").bitcast(F)
        w3_raw = pt_lo[:, :, :].rearrange("p a n -> p (a n)").bitcast(F)
        G_flat = G[:, :, :, :].rearrange("p b h k -> p (b h k)")
        NF = NB * NK * DC // 128
        flat = G_flat[:, GB * HK:GB * HK + NF]
        w2 = P_flat[:, 0:FP].rearrange("p (c n) -> p c n", c=FC)
        NT = GB * NQ
        hid = G_flat[:, 0:FC * NT].rearrange("p (c n) -> p c n", c=FC)
        silu = G_flat[:, FC * NT:FC * NT + 2 * NT].rearrange("p (c n) -> p c n", c=2)
        gated = G_flat[:, (FC + 2) * NT:(FC + 4) * NT].rearrange("p (c n) -> p c n", c=2)
        x2T_hi, x2T_lo = a_hi, a_lo
        y2 = O[:, :, :].rearrange("p a n -> p (a n)")
        x2 = y2[:, 0:NT].rearrange("p (b n) -> p b n", b=GB)
        lgT = y2[0:E, NT:2 * NT]
        small = y2[:, 2 * NT:4 * NT]
        gate_rows = OT[:, 0, :, :].rearrange("p c n -> p (c n)")[:, 0:GB * 128]\
            .rearrange("p (b n) -> p b n", b=GB)
        gT = sb("gT", [128, 2 * NT], BF)

        SB = [bank(f"S{p}") for p in range(3)]
        QB = [bank(f"Q{p}") for p in range(2)]
        WB = [bank(f"W{p}") for p in range(3)]

        names = ("ld_x0 ld_x1 ld_x2 ld_ctx ld_ctx_rest ld_flat ld_qk ld_wv ld_wo ld_w1 ld_w3 ld_rw ld_id ld_sel ld_w2 ld_bo "
                 "ld_rank st_out amax_done amax_all scale_step wv_lo_done wo_done a_mm a_hi_done a_lo_done wv_hi_done "
                 "w1_hi_done w3_hi_done rw_hi_done w_lo_done half_set ones_set pt_zero "
                 "s_S s_V s_G s_O s_PT s_T s_out s_xT "
                 "a_G a_Vhi a_exp a_PThi a_T a_xT a_cg a_cv "
                 "d_max d_sub d_Vlo d_rec d_On d_PTlo d_res d_bn d_aggr d_xln d_cg d_cv p_ve p_rstd p_xb "
                 "b_x2T b_lgT b_lg b_gT b_a b_b b_g b_y "
                 "c_x2hi c_lgT c_gT c_silu v_x2lo v_bn v_aggr v_x2 v_gate v_step v_gated v_hid v_out q_rstd q_ve gt_zero").split()
        s = {n: sem(n) for n in names}

        FIRST, LOOP0, LOOP1, LAST = -4, 4, NB - GB, NB
        def on(t, lo, hi):
            return not isinstance(t, int) or lo <= t < hi

        def at_slot(t, *which):
            return isinstance(t, int) and t in which

        def wait(eng, name, value):
            if not isinstance(value, int) or value > 0:
                eng.wait_ge(s[name], value)

        def apart(eng):
            eng.nop(nofuse=True)

        def slots(eng, slot):
            for t in range(FIRST, LOOP0):
                slot(t, t % GB)
            with eng.Fori(1, LOOP1 // GB) as g:
                for j in range(GB):
                    slot(g * GB + j, j)
            for t in range(LOOP1, LAST + 1):
                slot(t, t % GB)

        block = stack.enter_context(nc.Block())

        @block.sync
        def _(sp):
            sp.dma_start(wk_raw[:, 0:H * DC], wk_d).then_inc(s["ld_qk"], 16)
            sp.dma_start(wq_raw, wq_d).then_inc(s["ld_qk"], 16)
            sp.dma_start(ctx_raw[:, 0:GB * NK], ctx_d[:, 0:GB * NK]).then_inc(s["ld_ctx"], 16)
            sp.dma_start(ident[:, :], ident_d).then_inc(s["ld_id"], 16)
            sp.dma_start(X[:, 0:GB, :], x_d[:, 0:GB, :]).then_inc(s["ld_x0"], 16)
            sp.dma_start(flat, ctxflat_d).then_inc(s["ld_flat"], 16)
            sp.dma_start(wv_raw, wv_d).then_inc(s["ld_wv"], 16)
            sp.dma_start(wo_raw, wo_d).then_inc(s["ld_wo"], 16)
            sp.dma_start(bo[:, :], bo_d).then_inc(s["ld_bo"], 16)
            sp.dma_start(ctx_raw[:, GB * NK:], ctx_d[:, GB * NK:]).then_inc(s["ld_ctx_rest"], 16)
            sp.dma_start(w1_raw[:, 0:FP], w1_d).then_inc(s["ld_w1"], 16)
            sp.dma_start(w3_raw[:, 0:FP], w3_d).then_inc(s["ld_w3"], 16)
            sp.dma_start(rw[:, :], rw_d).then_inc(s["ld_rw"], 16)
            sp.dma_start(rank[:, :, :], rank_d).then_inc(s["ld_rank"], 16)
            sp.dma_start(X[:, GB:2 * GB, :], x_d[:, GB:2 * GB, :]).then_inc(s["ld_x1"], 16)
            sp.dma_start(X[:, 2 * GB:, :], x_d[:, 2 * GB:, :]).then_inc(s["ld_x2"], 16)
            sp.wait_ge(s["s_PT"], 4 * NB)
            sp.dma_start(w2, w2_d).then_inc(s["ld_w2"], 16)
            with sp.Fori(0, NG) as g:
                sp.wait_ge(s["v_out"], g + 1)
                sp.dma_start(out_d[:, ds(g * GB, GB), :], X[:, ds(g * GB, GB), :]).then_inc(s["st_out"], 16)
            sp.wait_ge(s["st_out"], 16 * NG)

        @block.gpsimd
        def _(pool):
            pool.dma_start(sel[:, :], sel_d).then_inc(s["ld_sel"], 16)
            pool.memset(half[:, :], -0.5).then_inc(s["half_set"], 1)
            for c in range(2):
                pool.wait_ge(s["amax_done"], c + 1)
                nc.gpsimd.partition_all_reduce(amall[:, c:c + 1], amax[:, c:c + 1], 128,
                                               bass.bass_isa.ReduceOp.max).then_inc(s["amax_all"], 1)
            pool.wait_ge(s["ld_bo"], 16)
            pool.wait_ge(s["half_set"], 1)

            def slot(t, j):
                if on(t, -2, NB - 2):
                    wait(pool, "d_aggr", t + 3)
                    apart(pool)
                    pool.tensor_scalar(ve[:, 0:1], mv[:, j % 2, 1:2], EPS, 1.0, ALU.add, ALU.mult).then_inc(s["p_ve"], 1)
                    pool.wait_ge(s["p_ve"], t + 3)
                    pool.tensor_tensor(rstd[:, j % 2:j % 2 + 1], ve[:, 0:1], half[:, 0:1], ALU.pow).then_inc(s["p_rstd"], 1)
                if on(t, 0, NB):
                    if isinstance(t, int):
                        pool.wait_ge(s[("ld_x0", "ld_x1", "ld_x2")[min(t // GB, 2)]], 16)
                    if at_slot(t, LOOP0 - 1):
                        pool.wait_ge(s["ld_x2"], 16)
                    wait(pool, "d_res", t - 1)
                    pool.tensor_tensor(xb[:, j % 2:j % 2 + 1, :], X[:, ds(t, 1), :], bo[:, :].rearrange("p (a n) -> p a n", a=1),
                                       ALU.add).then_inc(s["p_xb"], 1)
            slots(pool, slot)

            with pool.Fori(0, NG) as g:
                pool.wait_ge(s["v_aggr"], g + 1)
                apart(pool)
                pool.tensor_scalar(ve[:, 0:4], small[:, 1:2 * GB:2], EPS, 1.0, ALU.add, ALU.mult).then_inc(s["q_ve"], 1)
                pool.wait_ge(s["q_ve"], g + 1)
                pool.tensor_tensor(small[:, 8:8 + GB], ve[:, 0:4], half[:, :], ALU.pow).then_inc(s["q_rstd"], 1)

        @block.scalar
        def _(act):
            for q in range(4):
                act.wait_ge(s["a_mm"], q + 1)
                act.activation(a_hi[0:DC, q * 512:(q + 1) * 512], [*SB, QB[0]][q][0:DC, :], ACT.Copy,
                               scale=DH ** -0.5).then_inc(s["a_hi_done"], 1)

            def slot(t, j):
                if on(t, FIRST, NB - GB) and j == 0:
                    if isinstance(t, int):
                        act.wait_ge(s["ld_ctx" if t == FIRST else "ld_ctx_rest"], 16)
                    wait(act, "s_G", 4 * (t + 4))
                    apart(act)
                    act.activation(cg_hi[:, :], ctx_raw[:, ds((t + 4) * NK, GB * NK)], ACT.Copy).then_inc(s["a_cg"], 1)
                if on(t, -1, NB - 1):
                    wait(act, "s_V", 2 * t)
                    apart(act)
                    act.activation(cv_hi[:, (j + 1) % 2, :], ctx_raw[:, ds((t + 1) * NK, NK)], ACT.Copy).then_inc(s["a_cv"], 1)

                def v_high(k):
                    wait(act, "s_V", 2 * t + k + 1)
                    if k == 0:
                        wait(act, "s_O", 3 * (t - 1))
                    act.activation(v_hi[0:NK, j % 2, 8 * k:8 * k + 8, 0:DH],
                                   WB[k][0:NK, :].rearrange("p (h n) -> p h n", h=8), ACT.Copy).then_inc(s["a_Vhi"], 1)

                def exps(p):
                    lo, hi = SP[p]
                    wait(act, "d_sub", 3 * t + p + 1)
                    act.activation(P[:, j % 2, lo * NK:hi * NK], P[:, j % 2, lo * NK:hi * NK], ACT.Exp).then_inc(s["a_exp"], 1)

                def g_out(k):
                    wait(act, "s_G", 4 * (t + 4) + k + 1)
                    if k == 0 and j == 0:
                        wait(act, "s_S", 3 * t)
                    half_ = (t // GB + 1) % 2 if isinstance(t, int) else ((t + 4) // GB) % 2
                    apart(act)
                    act.activation(G[:, ds(half_ * GB, GB), 4 * j + k, :],
                                   WB[(2, 0, 1, 2)[k]][:, 0:GB * NK].rearrange("p (b n) -> p b n", b=GB),
                                   ACT.Copy).then_inc(s["a_G"], 1)

                def pt_high(c):
                    wait(act, "s_PT", 4 * t + c + 1)
                    if c == 0:
                        wait(act, "s_O", 3 * (t - 1))
                        if at_slot(t, 0, 1):
                            act.wait_ge(s["pt_zero"], 1)
                    act.activation(pt_hi[0:NK, j % 2, c * 512:(c + 1) * 512], QB[(5 * j + c) % 2][0:NK, :],
                                   ACT.Copy).then_inc(s["a_PThi"], 1)

                def oT(k):
                    wait(act, "s_T", 2 * (t - 1) + k + 1)
                    wait(act, "s_out", t - 2)
                    act.activation(OT[:, (j + 1) % 2, 4 * k:4 * k + 4, :],
                                   WB[k][:, :].rearrange("p (c n) -> p c n", c=4), ACT.Copy).then_inc(s["a_T"], 1)

                now, gon, old = on(t, 0, NB), on(t, FIRST, NB - GB), on(t, 1, NB + 1)
                if now:
                    v_high(0); exps(0); v_high(1); exps(1)
                if gon:
                    g_out(0)
                if now:
                    exps(2)
                if gon:
                    g_out(1)
                if now:
                    pt_high(0)
                if gon:
                    g_out(2)
                if now:
                    pt_high(1)
                if gon:
                    g_out(3)
                if old:
                    oT(0); oT(1)
                if now:
                    pt_high(2); pt_high(3)
                if on(t, -1, NB - 1):
                    wait(act, "s_xT", t + 2)
                    wait(act, "s_S", 3 * t)
                    act.activation(xT[:, (j + 1) % 2, :], QB[(5 * j + 4) % 2][:, 0:NQ], ACT.Copy).then_inc(s["a_xT"], 1)
                if at_slot(t, FIRST):
                    act.wait_ge(s["scale_step"], 6)
                    act.wait_ge(s["ld_wv"], 16)
                    act.activation(wv_hi[:, :], wv_raw, ACT.Copy, scale=sc[0:DC, 4:5]).then_inc(s["wv_hi_done"], 1)
                    act.wait_ge(s["ld_wo"], 16)
                    act.activation(wo[:, :, :], wo_raw.rearrange("p (c n) -> p c n", c=8), ACT.Copy,
                                   scale=sc[:, 5:6]).then_inc(s["wo_done"], 1)
                    for w, (hi, raw) in {"w1": (w1_hi, w1_raw), "w3": (w3_hi, w3_raw)}.items():
                        act.wait_ge(s["ld_" + w], 16)
                        act.activation(hi[:, :], raw[:, 0:FP], ACT.Copy).then_inc(s[w + "_hi_done"], 1)
                    act.wait_ge(s["ld_rw"], 16)
                    act.activation(rw_hi[:, :], rw[:, :], ACT.Copy).then_inc(s["rw_hi_done"], 1)
            slots(act, slot)

            def x2_high(g):
                act.wait_ge(s["b_x2T"], g + 1)
                wait(act, "b_b", FC * (g - 1))
                apart(act)
                act.activation(x2T_hi[:, ds(g % 2 * NT, NT)], QB[1][:, :], ACT.Copy).then_inc(s["c_x2hi"], 1)

            def logits_out(g):
                act.wait_ge(s["b_lgT"], g + 1)
                act.activation(lgT, QB[1][0:E, :], ACT.Copy).then_inc(s["c_lgT"], 1)

            def gates_out(g):
                act.wait_ge(s["b_gT"], g + 1)
                apart(act)
                act.activation(gT[:, ds(g % 2 * NT, NT)], QB[1][:, :], ACT.Copy).then_inc(s["c_gT"], 1)

            def chunk(g, c):
                act.wait_ge(s["b_a"], FC * g + c + 1)
                wait(act, "v_gated", FC * g + max(c - 1, 0))
                act.activation(silu[:, c % 2, :], SB[c % 2][:, :], ACT.Silu).then_inc(s["c_silu"], 1)

            def group(g, more):
                for c in range(FC):
                    chunk(g, c)
                    if more and c == 3:
                        x2_high(g + 1)
                    if more and c == 5:
                        logits_out(g + 1)
                    if more and c == 11:
                        gates_out(g + 1)

            act.wait_ge(s["s_S"], 3 * NB)
            x2_high(0)
            logits_out(0)
            gates_out(0)
            group(0, True)
            with act.Fori(1, NG - 1) as g:
                group(g, True)
            group(NG - 1, False)

        @block.vector
        def _(dve):
            dve.wait_ge(s["ld_flat"], 16)
            dve.tensor_reduce(amax[:, 0:1], flat, AX.X, ALU.max, apply_absolute_value=True).then_inc(s["amax_done"], 1)
            dve.memset(amax[:, 1:2], 0.0).then_inc(s["scale_step"], 1)
            dve.wait_ge(s["scale_step"], 1)
            dve.wait_ge(s["ld_wv"], 16)
            dve.tensor_reduce(amax[0:DC, 1:2], wv_raw, AX.X, ALU.max, apply_absolute_value=True).then_inc(s["amax_done"], 1)
            for q in range(4):
                dve.wait_ge(s["a_hi_done"], q + 1)
                dve.scalar_tensor_tensor(a_lo[0:DC, q * 512:(q + 1) * 512], [*SB, QB[0]][q][0:DC, :], DH ** -0.5,
                                         a_hi[0:DC, q * 512:(q + 1) * 512].bitcast(F), ALU.mult,
                                         ALU.subtract).then_inc(s["a_lo_done"], 1)
            dve.wait_ge(s["amax_all"], 2)
            dve.tensor_scalar(sc[:, 0:2], amall[:, :], TINY, None, ALU.max).then_inc(s["scale_step"], 1)
            dve.wait_ge(s["scale_step"], 2)
            dve.tensor_scalar(sc[:, 2:4].bitcast(U), sc[:, 0:2].bitcast(U), 0x7F800000, None,
                              ALU.bitwise_and).then_inc(s["scale_step"], 1)
            dve.wait_ge(s["scale_step"], 3)
            dve.tensor_scalar(sc[:, 5:6], sc[:, 2:3], sc[:, 3:4], 1.0 / VBOOST, ALU.mult, ALU.mult).then_inc(s["scale_step"], 1)
            dve.reciprocal(sc[:, 6:8], sc[:, 2:4]).then_inc(s["scale_step"], 1)
            dve.wait_ge(s["scale_step"], 5)
            dve.tensor_scalar(sc[:, 4:5], sc[:, 6:7], sc[:, 7:8], VBOOST, ALU.mult, ALU.mult).then_inc(s["scale_step"], 1)
            dve.memset(v_lo[:, :, :, :], 0.0).then_inc(s["ones_set"], 1)
            dve.memset(v_hi[:, :, :, :], 1.0).then_inc(s["ones_set"], 1)

            def slot(t, j):
                if on(t, FIRST, NB - GB) and j == 0:
                    wait(dve, "a_cg", t // GB + 2 if isinstance(t, int) else (t + 8) // GB)
                    dve.tensor_tensor(cg_lo[:, :], ctx_raw[:, ds((t + 4) * NK, GB * NK)], cg_hi[:, :].bitcast(F),
                                      ALU.subtract).then_inc(s["d_cg"], 1)
                if on(t, -1, NB - 1):
                    wait(dve, "a_cv", t + 2)
                    dve.tensor_tensor(cv_lo[:, (j + 1) % 2, :], ctx_raw[:, ds((t + 1) * NK, NK)],
                                      cv_hi[:, (j + 1) % 2, :].bitcast(F), ALU.subtract).then_inc(s["d_cv"], 1)
                    wait(dve, "p_rstd", t + 2)
                    wait(dve, "s_xT", t)
                    k = (j + 1) % 2
                    dve.tensor_scalar(xln[:, k:k + 1, :], X[:, ds(t + 1, 1), :], mv[:, k, 0:1], rstd[:, k:k + 1],
                                      ALU.subtract, ALU.mult).then_inc(s["d_xln"], 1)

                def piece_max(p):
                    lo, hi = SP[p]
                    wait(dve, "s_S", 3 * t + p + 1)
                    dve.tensor_reduce(top[:, j % 2, lo:hi], SB[p][:, 0:(hi - lo) * NK].rearrange("p (h k) -> p h k", k=NK),
                                      AX.X, ALU.max).then_inc(s["d_max"], 1)

                def piece_sub(p):
                    lo, hi = SP[p]
                    wait(dve, "d_max", 3 * t + p + 1)
                    if p == 0:
                        wait(dve, "s_PT", 4 * (t - 1))
                        if at_slot(t, 0, 1):
                            dve.wait_ge(s["wv_lo_done"], 1)
                            dve.wait_ge(s["wo_done"], 1)
                    dve.tensor_tensor(P[:, j % 2, lo * NK:hi * NK].rearrange("p (h k) -> p h k", k=NK),
                                      SB[p][:, 0:(hi - lo) * NK].rearrange("p (h k) -> p h k", k=NK),
                                      top[:, j % 2, lo:hi].unsqueeze(2).broadcast_to([128, hi - lo, NK]),
                                      ALU.subtract).then_inc(s["d_sub"], 1)

                def v_low(k):
                    wait(dve, "a_Vhi", 2 * t + k + 1)
                    dve.tensor_tensor(v_lo[0:NK, j % 2, 8 * k:8 * k + 8, 0:DH],
                                      WB[k][0:NK, :].rearrange("p (h n) -> p h n", h=8),
                                      v_hi[0:NK, j % 2, 8 * k:8 * k + 8, 0:DH], ALU.subtract).then_inc(s["d_Vlo"], 1)

                def piece(p):
                    lo, hi = OP[p]
                    return SB[p][:, 0:(hi - lo) * (DH + 1)].rearrange("p (h n) -> p h n", n=DH + 1)

                def sums(p):
                    lo, hi = OP[p]
                    wait(dve, "s_O", 3 * (t - 1) + p + 1)
                    dve.reciprocal(rec[:, (j + 1) % 2, lo:hi].unsqueeze(2), piece(p)[:, :, DH:DH + 1]).then_inc(s["d_rec"], 1)

                def normed(p):
                    lo, hi = OP[p]
                    wait(dve, "d_rec", 3 * (t - 1) + p + 1)
                    wait(dve, "s_T", 2 * (t - 2))
                    dve.tensor_tensor(O[:, (j + 1) % 2, lo * DH:hi * DH].rearrange("p (h n) -> p h n", n=DH),
                                      piece(p)[:, :, 0:DH],
                                      rec[:, (j + 1) % 2, lo:hi].unsqueeze(2).broadcast_to([128, hi - lo, DH]),
                                      ALU.mult).then_inc(s["d_On"], 1)

                def pt_low(c):
                    wait(dve, "a_PThi", 4 * t + c + 1)
                    dve.tensor_tensor(pt_lo[0:NK, j % 2, c * 512:(c + 1) * 512], QB[(5 * j + c) % 2][0:NK, :],
                                      pt_hi[0:NK, j % 2, c * 512:(c + 1) * 512], ALU.subtract).then_inc(s["d_PTlo"], 1)

                if on(t, 0, NB):
                    piece_max(0); piece_max(1); piece_sub(0); piece_max(2); piece_sub(1); piece_sub(2)
                    v_low(0); v_low(1)
                if on(t, 1, NB + 1):
                    sums(0); sums(1); normed(0); sums(2); normed(1); normed(2)
                if on(t, 0, NB):
                    pt_low(0); pt_low(1); pt_low(2)
                if on(t, -2, NB - 2):
                    if isinstance(t, int):
                        dve.wait_ge(s[("ld_x0", "ld_x1", "ld_x2")[min((t + 2) // GB, 2)]], 16)
                    if at_slot(t, LOOP0 - 1):
                        dve.wait_ge(s["ld_x2"], 16)
                    dve.bn_stats(bn[:, :], X[:, ds(t + 2, 1), :].rearrange("p a n -> p (a n)")).then_inc(s["d_bn"], 1)
                    dve.wait_ge(s["d_bn"], t + 3)
                    apart(dve)
                    dve.bn_aggr(mv[:, j % 2, :], bn[:, :]).then_inc(s["d_aggr"], 1)
                if on(t, 1, NB + 1):
                    wait(dve, "s_out", t)
                    wait(dve, "p_xb", t)
                    dve.tensor_tensor(X[:, ds(t - 1, 1), :], WB[2][:, 0:D].rearrange("p (a n) -> p a n", a=1),
                                      xb[:, (j + 1) % 2:(j + 1) % 2 + 1, :], ALU.add).then_inc(s["d_res"], 1)
                if on(t, 0, NB):
                    pt_low(3)
                if at_slot(t, FIRST):
                    dve.wait_ge(s["wv_hi_done"], 1)
                    dve.scalar_tensor_tensor(wv_lo[:, :], wv_raw, sc[0:DC, 4:5], wv_hi[:, :].bitcast(F), ALU.mult,
                                             ALU.subtract).then_inc(s["wv_lo_done"], 1)
                    for w, hi, lo, raw in (("w1", w1_hi, w1_lo, w1_raw), ("w3", w3_hi, w3_lo, w3_raw)):
                        dve.wait_ge(s[w + "_hi_done"], 1)
                        dve.tensor_tensor(lo[:, :], raw[:, 0:FP], hi[:, :].bitcast(F), ALU.subtract).then_inc(s["w_lo_done"], 1)
                    dve.wait_ge(s["rw_hi_done"], 1)
                    dve.tensor_tensor(rw_lo[:, :], rw[:, :], rw_hi[:, :].bitcast(F), ALU.subtract).then_inc(s["w_lo_done"], 1)
                    dve.wait_ge(s["w_lo_done"], 3)
                    dve.memset(pt_hi[64:KR, :, :], 0.0)
                    dve.memset(pt_lo[64:KR, :, :], 0.0).then_inc(s["pt_zero"], 1)
            slots(dve, slot)

            steps = []

            def step(ins, g):
                ins.then_inc(s["v_step"], 1)
                steps.append(1)
                dve.wait_ge(s["v_step"], g * STEPS + len(steps))

            STEPS = 16

            def norm(g):
                wait(dve, "b_x2T", g)
                for i in range(GB):
                    dve.bn_stats(small[:, 16 + 6 * i:22 + 6 * i],
                                 X[:, ds(g * GB + i, 1), :].rearrange("p a n -> p (a n)")).then_inc(s["v_bn"], 1)
                dve.wait_ge(s["v_bn"], GB * (g + 1))
                apart(dve)
                for i in range(GB):
                    last = dve.bn_aggr(small[:, 2 * i:2 * i + 2], small[:, 16 + 6 * i:22 + 6 * i])
                last.then_inc(s["v_aggr"], 1)
                dve.wait_ge(s["v_aggr"], g + 1)
                dve.wait_ge(s["q_rstd"], g + 1)
                for i in range(GB):
                    last = dve.tensor_scalar(x2[:, i:i + 1, :], X[:, ds(g * GB + i, 1), :], small[:, 2 * i:2 * i + 1],
                                             small[:, 8 + i:9 + i], ALU.subtract, ALU.mult)
                last.then_inc(s["v_x2"], 1)

            def x2_low(g):
                dve.wait_ge(s["c_x2hi"], g + 1)
                dve.tensor_tensor(x2T_lo[:, ds(g % 2 * NT, NT)], QB[1][:, :], x2T_hi[:, ds(g % 2 * NT, NT)].bitcast(F),
                                  ALU.subtract).then_inc(s["v_x2lo"], 1)

            def gates(g):
                steps.clear()
                dve.wait_ge(s["b_lg"], g + 1)
                at = [64 + 32 * i for i in range(8)]
                tile = lambda n: small[:, at[n]:at[n] + GB * E].rearrange("p (b e) -> p b e", e=E)
                one = lambda n: small[:, 48 + 4 * n:52 + 4 * n]
                wide = lambda n: one(n).unsqueeze(2).broadcast_to([128, GB, E])
                lg, eq, pick, pick2, rest = tile(0), tile(1), tile(2), tile(3), tile(4)
                step(dve.tensor_copy(lg, QB[1][:, 0:GB * E].rearrange("p (b e) -> p b e", e=E)), g)

                def largest(of, into):
                    step(dve.tensor_reduce(one(0), of, AX.X, ALU.max), g)
                    step(dve.tensor_tensor(eq, of, wide(0), ALU.is_equal), g)
                    step(dve.tensor_tensor(eq, eq, rank[:, :, :], ALU.mult), g)
                    step(dve.tensor_reduce(one(1), eq, AX.X, ALU.max), g)
                    step(dve.tensor_tensor(into, eq, wide(1), ALU.is_equal), g)

                largest(lg, pick)
                step(dve.scalar_tensor_tensor(rest, pick, -BIG, lg, ALU.mult, ALU.add), g)
                largest(rest, pick2)
                step(dve.tensor_tensor(pick, pick, pick2, ALU.add), g)
                step(dve.tensor_tensor(pick, pick, lg, ALU.mult), g)
                wait(dve, "b_gT", g)
                part, down = tile(5), tile(6)
                hi, mid, lo = (gate_rows[:, :, GR * n:GR * n + E] for n in range(3))
                bf = small[:, at[7]:at[7] + GB * E // 2].bitcast(BF).rearrange("p (b e) -> p b e", e=E)
                step(dve.tensor_copy(bf, pick), g)
                step(dve.tensor_copy(hi, bf), g)
                assert len(steps) == STEPS
                dve.tensor_tensor(part, pick, hi, ALU.subtract).then_inc(s["v_gate"], 1)
                dve.wait_ge(s["v_gate"], 5 * g + 1)
                dve.tensor_copy(bf, part).then_inc(s["v_gate"], 1)
                dve.wait_ge(s["v_gate"], 5 * g + 2)
                dve.tensor_copy(mid, bf).then_inc(s["v_gate"], 1)
                dve.wait_ge(s["v_gate"], 5 * g + 3)
                dve.tensor_tensor(down, part, mid, ALU.subtract).then_inc(s["v_gate"], 1)
                dve.wait_ge(s["v_gate"], 5 * g + 4)
                dve.tensor_copy(lo, down).then_inc(s["v_gate"], 1)

            def chunk(g, c):
                dve.wait_ge(s["c_silu"], FC * g + c + 1)
                dve.wait_ge(s["b_g"], FC * g + c + 1)
                dve.tensor_tensor(gated[:, c % 2, :], WB[c % 2][:, :], silu[:, c % 2, :], ALU.mult).then_inc(s["v_gated"], 1)
                dve.wait_ge(s["v_gated"], FC * g + c + 1)
                dve.wait_ge(s["b_b"], FC * g + c + 1)
                wait(dve, "b_y", FC * (g - 1) + c + 1)
                dve.tensor_tensor(hid[:, c, :], (SB[2], QB[0])[c % 2][:, :], gated[:, c % 2, :], ALU.mult).then_inc(s["v_hid"], 1)

            def group(g, more):
                for c in range(FC):
                    chunk(g, c)
                    if more and c == 1:
                        norm(g + 1)
                    if more and c == 3:
                        x2_low(g + 1)
                    if more and c == 8:
                        gates(g + 1)
                    if c == 0:
                        if not isinstance(g, int) or g > 0:
                            result(g - 1)

            def result(g):
                dve.wait_ge(s["b_y"], FC * (g + 1))
                dve.tensor_tensor(X[:, ds(g * GB, GB), :], WB[2][:, :].rearrange("p (b n) -> p b n", b=GB),
                                  X[:, ds(g * GB, GB), :], ALU.add).then_inc(s["v_out"], 1)

            dve.wait_ge(s["s_out"], NB)
            dve.memset(gate_rows, 0.0).then_inc(s["gt_zero"], 1)
            dve.wait_ge(s["gt_zero"], 1)
            dve.memset(gate_rows[:, :, E:E + 1], 1.0).then_inc(s["gt_zero"], 1)
            dve.wait_ge(s["ld_rank"], 16)
            dve.wait_ge(s["d_res"], NB)
            norm(0)
            x2_low(0)
            dve.wait_ge(s["gt_zero"], 2)
            gates(0)
            group(0, True)
            with dve.Fori(1, NG - 1) as g:
                group(g, True)
            group(NG - 1, False)
            result(NG - 1)

        @block.tensor
        def _(pe):
            pe.wait_ge(s["ld_qk"], 32)
            for q in range(4):
                for i in range(4):
                    h = 4 * q + i
                    last = pe.matmul([*SB, QB[0]][q][0:DC, i * D:(i + 1) * D], wk_raw[:, h * DC:(h + 1) * DC],
                                     wq_raw[:, h * D:(h + 1) * D], start=True, stop=True)
                last.then_inc(s["a_mm"], 1)
            pe.wait_ge(s["a_lo_done"], 4)
            pe.wait_ge(s["ld_id"], 16)

            def three(out, w_hi, w_lo, m_hi, m_lo):
                pe.matmul(out, w_hi, m_hi, start=True, stop=False)
                pe.matmul(out, w_hi, m_lo, start=False, stop=False)
                return pe.matmul(out, w_lo, m_hi, start=False, stop=True)

            def slot(t, j):
                def scores():
                    wait(pe, "a_xT", t + 1)
                    wait(pe, "a_G", 4 * (t - j) + 16)
                    half_ = (t // GB) % 2 if isinstance(t, int) else (t // GB) % 2
                    for p, (lo, hi) in enumerate(SP):
                        wait(pe, "d_On", 3 * (t - 2) + p + 1)
                        pe.matmul(SB[p][:, 0:(hi - lo) * NK], xT[:, j % 2, :],
                                  G_flat[:, ds((half_ * GB + j) * HK + lo * NK, (hi - lo) * NK)],
                                  start=True, stop=True).then_inc(s["s_S"], 1)

                def values(k):
                    wait(pe, "d_cv", t + 1)
                    wait(pe, "a_T", 2 * (t - 2) + k + 1)
                    if at_slot(t, 0):
                        pe.wait_ge(s["wv_lo_done"], 1)
                        pe.wait_ge(s["a_G"], 16)
                    cols = slice(k * 512, (k + 1) * 512)
                    three(WB[k][0:NK, :], cv_hi[:, j % 2, :], cv_lo[:, j % 2, :], wv_hi[:, cols],
                          wv_lo[:, cols]).then_inc(s["s_V"], 1)

                def g_piece(k):
                    if k == 0:
                        wait(pe, "d_cg", t // GB + 2 if isinstance(t, int) else (t + 8) // GB)
                        wait(pe, "d_res", t - 1)
                        wait(pe, "a_G", 4 * (t + 4))
                    elif k < 3:
                        if on(t, 0, NB):
                            wait(pe, "d_Vlo", 2 * t + k)
                    else:
                        wait(pe, "a_G", 4 * (t + 4) + 1)
                    h = 4 * j + k
                    three(WB[(2, 0, 1, 2)[k]][:, 0:GB * NK], a_hi[0:DC, h * D:(h + 1) * D], a_lo[0:DC, h * D:(h + 1) * D],
                          cg_hi[:, :], cg_lo[:, :]).then_inc(s["s_G"], 1)

                def pv(p):
                    lo, hi = OP[p]
                    b = (j + 1) % 2
                    if on(t, 0, NB):
                        wait(pe, "d_sub", 3 * t + p + 1)
                    else:
                        wait(pe, "d_On", 3 * (t - 2) + p + 1)
                    if p == 0:
                        wait(pe, "d_PTlo", 4 * t)
                        wait(pe, "d_Vlo", 2 * t)
                        if at_slot(t, 1):
                            pe.wait_ge(s["ones_set"], 2)
                    for i, h in enumerate(range(lo, hi)):
                        out = SB[p][:, i * (DH + 1):(i + 1) * (DH + 1)]
                        ph, pl = (w[0:KR, b, h * NQ:(h + 1) * NQ] for w in (pt_hi, pt_lo))
                        pe.matmul(out, ph, v_hi[:, b, h, :], start=True, stop=False)
                        pe.matmul(out, ph, v_lo[:, b, h, :], start=False, stop=False)
                        last = pe.matmul(out, pl, v_hi[:, b, h, :], start=False, stop=True)
                    last.then_inc(s["s_O"], 1)

                def p_turn(c):
                    wait(pe, "a_exp", 3 * t + (1, 2, 2, 3)[c])
                    if c == 0:
                        wait(pe, "d_PTlo", 4 * t)
                    elif c == 1:
                        wait(pe, "a_xT", t + 1)
                    else:
                        wait(pe, "d_PTlo", 4 * t + c - 1)
                    for i in range(4):
                        h = 4 * c + i
                        last = pe.transpose(QB[(5 * j + c) % 2][0:NK, i * NQ:(i + 1) * NQ],
                                            P[:, j % 2, h * NK:(h + 1) * NK], ident[:, :])
                    last.then_inc(s["s_PT"], 1)

                def o_turn(k):
                    wait(pe, "d_On", 3 * (t - 1) + k + 2)
                    if on(t, FIRST, NB - GB):
                        wait(pe, "a_G", 4 * (t + 4) + k + 2)
                    elif on(t, 0, NB):
                        wait(pe, "d_Vlo", 2 * t + k + 1)
                    else:
                        wait(pe, "a_T", 2 * (t - 2) + k + 1)
                    for i in range(4):
                        c = 4 * k + i
                        last = pe.transpose(WB[k][:, i * NQ:(i + 1) * NQ], O[:, (j + 1) % 2, c * 128:(c + 1) * 128], ident[:, :])
                    last.then_inc(s["s_T"], 1)

                def project():
                    wait(pe, "a_T", 2 * t)
                    if on(t, FIRST, NB - GB):
                        wait(pe, "a_G", 4 * (t + 4) + 4)
                    else:
                        wait(pe, "d_res", t - 1)
                    if at_slot(t, 1):
                        pe.wait_ge(s["wo_done"], 1)
                    for c in range(8):
                        last = pe.matmul(WB[2][:, 0:D], OT[:, (j + 1) % 2, c, :], wo[:, c, :], start=(c == 0), stop=(c == 7))
                    last.then_inc(s["s_out"], 1)

                now, gon, old = on(t, 0, NB), on(t, FIRST, NB - GB), on(t, 1, NB + 1)
                if now:
                    scores(); values(0); values(1)
                if gon:
                    g_piece(0)
                if old:
                    pv(0); pv(1); pv(2)
                if gon:
                    g_piece(1)
                if now:
                    p_turn(0)
                if gon:
                    g_piece(2)
                if now:
                    p_turn(1)
                if gon:
                    g_piece(3)
                if old:
                    o_turn(0); o_turn(1)
                if now:
                    p_turn(2)
                if old:
                    project()
                if now:
                    p_turn(3)
                if on(t, -1, NB - 1):
                    wait(pe, "d_xln", t + 2)
                    wait(pe, "d_PTlo", 4 * t + 3)
                    pe.transpose(QB[(5 * j + 4) % 2][:, 0:NQ], xln[:, (j + 1) % 2, :], ident[:, :]).then_inc(s["s_xT"], 1)
            slots(pe, slot)

            def x2_turn(g):
                pe.wait_ge(s["v_x2"], g + 1)
                wait(pe, "c_gT", g)
                for i in range(GB):
                    last = pe.transpose(QB[1][:, i * NQ:(i + 1) * NQ], x2[:, i, :], ident[:, :])
                last.then_inc(s["b_x2T"], 1)

            def logits(g):
                pe.wait_ge(s["v_x2lo"], g + 1)
                at = ds(g % 2 * NT, NT)
                three(QB[1][0:E, :], rw_hi[:, :], rw_lo[:, :], x2T_hi[:, at], x2T_lo[:, at]).then_inc(s["b_lgT"], 1)

            def logits_turn(g):
                pe.wait_ge(s["c_lgT"], g + 1)
                apart(pe)
                for i in range(GB):
                    last = pe.transpose(QB[1][:, i * E:(i + 1) * E], lgT[:, i * NQ:(i + 1) * NQ], ident[0:E, 0:E])
                last.then_inc(s["b_lg"], 1)

            def gates_turn(g):
                pe.wait_ge(s["v_gate"], 5 * g + 5)
                for i in range(GB):
                    last = pe.transpose(QB[1][:, i * NQ:(i + 1) * NQ], gate_rows[:, i, :], ident[:, :])
                last.then_inc(s["b_gT"], 1)

            def up(g, c):
                at, cols = ds(g % 2 * NT, NT), slice(c * 128, (c + 1) * 128)
                before = FC * g + max(c - 1, 0)
                wait(pe, "c_silu", before)
                three(SB[c % 2][:, :], w1_hi[:, cols], w1_lo[:, cols], x2T_hi[:, at], x2T_lo[:, at]).then_inc(s["b_a"], 1)
                if c == 0:
                    pe.wait_ge(s["c_gT"], g + 1)
                wait(pe, "v_gated", before)
                pe.matmul(WB[c % 2][:, :], sel[:, cols], gT[:, at], start=True, stop=True).then_inc(s["b_g"], 1)
                wait(pe, "v_hid", before)
                three((SB[2], QB[0])[c % 2][:, :], w3_hi[:, cols], w3_lo[:, cols], x2T_hi[:, at], x2T_lo[:, at]).then_inc(s["b_b"], 1)

            def down(g, c):
                pe.wait_ge(s["v_hid"], FC * g + c + 1)
                if c == 0:
                    wait(pe, "v_out", g)
                for i in range(GB):
                    last = pe.matmul(WB[2][:, i * D:(i + 1) * D], hid[:, c, i * NQ:(i + 1) * NQ], w2[:, c, :],
                                     start=(c == 0 and i == 0), stop=(c == FC - 1), skip_group_check=True)
                last.then_inc(s["b_y"], 1)

            def group(g, more):
                for c in range(FC):
                    up(g, c)
                    if c >= 2:
                        down(g, c - 2)
                    if more and c == 3:
                        x2_turn(g + 1)
                    if more and c == 5:
                        logits(g + 1)
                    if more and c == 7:
                        logits_turn(g + 1)
                    if more and c == 11:
                        gates_turn(g + 1)
                down(g, FC - 2)
                down(g, FC - 1)

            pe.wait_ge(s["w_lo_done"], 3)
            pe.wait_ge(s["ld_sel"], 16)
            pe.wait_ge(s["ld_w2"], 16)
            pe.wait_ge(s["d_PTlo"], 4 * NB)
            pe.wait_ge(s["a_T"], 2 * NB)
            pe.wait_ge(s["d_On"], 3 * NB)
            pe.wait_ge(s["d_res"], NB)
            x2_turn(0)
            logits(0)
            logits_turn(0)
            gates_turn(0)
            group(0, True)
            with pe.Fori(1, NG - 1) as g:
                group(g, True)
            group(NG - 1, False)


def kernel(x, ctx_768, L0_xattn_w_q, L0_xattn_w_kv, L0_xattn_w_out, L0_xattn_b_out, L0_ffn_router_w,
           L0_ffn_w1, L0_ffn_w2, L0_ffn_w3, L0_ffn_sw1, L0_ffn_sw2, L0_ffn_sw3):
    import concourse.bacc as bacc
    from concourse.bass_utils import run_bass_kernel_spmd

    f = np.float32
    x, ctx = np.asarray(x), np.asarray(ctx_768)
    wq, wkv, wout, bout = (np.asarray(a) for a in (L0_xattn_w_q, L0_xattn_w_kv, L0_xattn_w_out, L0_xattn_b_out))
    w1, w2, w3 = (np.asarray(a) for a in (L0_ffn_w1, L0_ffn_w2, L0_ffn_w3))
    sw1, sw2, sw3 = (np.asarray(a) for a in (L0_ffn_sw1, L0_ffn_sw2, L0_ffn_sw3))
    inner = H * DH
    pad = np.zeros((FP - FU, D), f)
    sel = np.zeros((128, FP), f)
    for part in range(3):
        for e in range(E + 1):
            if e < E or part == 0:
                sel[part * GR + e, e * I:(e + 1) * I] = 1.0
    rank = np.broadcast_to(np.arange(E, 0, -1, dtype=f), (128, GB, E))
    arrays = {
        "x": x.transpose(1, 0, 2),
        "ctxT": ctx.transpose(2, 0, 1).reshape(DC, NB * NK),
        "ctx_flat": ctx.reshape(128, -1),
        "wqT": wq.reshape(D, H, DH).transpose(2, 1, 0).reshape(DH, H * D),
        "wkT": wkv[:, :inner].reshape(DC, H, DH).transpose(2, 1, 0).reshape(DH, H * DC),
        "wv": wkv[:, inner:],
        "wo": wout.reshape(8, 128, D).transpose(1, 0, 2).reshape(128, 8 * D),
        "bo": np.broadcast_to(bout, (128, D)),
        "rwT": np.asarray(L0_ffn_router_w).T,
        "w1T": np.concatenate([w1.reshape(E * I, D), sw1, pad]).T,
        "w3T": np.concatenate([w3.reshape(E * I, D), sw3, pad]).T,
        "w2": np.concatenate([w2.transpose(0, 2, 1).reshape(E * I, D), sw2.T, pad]).reshape(FC, 128, D).transpose(1, 0, 2),
        "sel": sel, "ident": np.eye(128, dtype=f), "rank": rank,
    }
    arrays = {n: np.ascontiguousarray(a) for n, a in arrays.items()}
    nc = bacc.Bacc("TRN2", target_bir_lowering=False, num_devices=1)
    ins = [nc.dram_tensor(n + "_in", a.shape, mybir.dt.from_np(a.dtype), kind="ExternalInput").ap() for n, a in arrays.items()]
    out = nc.dram_tensor("y_out", (128, NB, D), mybir.dt.float32, kind="ExternalOutput").ap()
    program(nc, *ins, out)
    got = run_bass_kernel_spmd(nc, [{n + "_in": a for n, a in arrays.items()}], core_ids=[0])
    return got.results[0]["y_out"].transpose(1, 0, 2)
```

```python
import numpy as np
import concourse.bass as bass
from concourse import mybir
from contextlib import ExitStack

NB, NQ, D = 64, 128, 128
NK, DC = 77, 96
H, DH = 16, 64
E, I, TOPK = 8, 176, 2
GB = 4
NG = NB // GB
HK = H * NK
KR = 96
FU = (E + 1) * I
FC = -(-FU // 128)
FP = FC * 128
SP = [(0, 6), (6, 12), (12, 16)]
OP = [(0, 6), (6, 11), (11, 16)]
GR = 16
EPS = 1e-5
VBOOST = 128.0
TINY = 2.0 ** -60
BIG = 3.0e38


def program(nc, x_d, ctx_d, ctxflat_d, wq_d, wk_d, wv_d, wo_d, bo_d, rw_d, w1_d, w3_d, w2_d, sel_d,
            ident_d, rank_d, out_d):
    F, R, HF, BF, U = (mybir.dt.float32, mybir.dt.float32r, mybir.dt.float16, mybir.dt.bfloat16,
                       mybir.dt.uint32)
    ACT, ALU, AX = mybir.ActivationFunctionType, mybir.AluOpType, mybir.AxisListType
    ds = bass.ds
    stack = ExitStack()
    with stack:
        def sb(name, shape, dt=F):
            return stack.enter_context(nc.sbuf_tensor(name, shape, dt))

        def bank(name):
            return stack.enter_context(nc.psum_tensor(name, [128, 512], F))

        def sem(name):
            return stack.enter_context(nc.semaphore(name))

        X = sb("X", [128, NB, D])
        ctx_raw = sb("ctx_raw", [DC, NB * NK])
        a_hi = sb("a_hi", [128, H * D], R)
        a_lo = sb("a_lo", [128, H * D], R)
        wv_hi = sb("wv_hi", [DC, H * DH], R)
        wv_lo = sb("wv_lo", [DC, H * DH], R)
        wo = sb("wo", [128, 8, D])
        G = sb("G", [128, 2 * GB, H, NK])
        cg_hi = sb("cg_hi", [DC, GB * NK], R)
        cg_lo = sb("cg_lo", [DC, GB * NK], R)
        cv_hi = sb("cv_hi", [DC, 2, NK], R)
        cv_lo = sb("cv_lo", [DC, 2, NK], R)
        xln = sb("xln", [128, 2, D])
        xT = sb("xT", [128, 2, NQ])
        P = sb("P", [128, 2, HK])
        pt_hi = sb("pt_hi", [128, 2, H * NQ], HF)
        pt_lo = sb("pt_lo", [128, 2, H * NQ], HF)
        v_hi = sb("v_hi", [KR, 2, H, DH + 1], HF)
        v_lo = sb("v_lo", [KR, 2, H, DH + 1], HF)
        O = sb("O", [128, 2, H * DH])
        OT = sb("OT", [128, 2, 8, NQ])
        xb = sb("xb", [128, 2, D])
        bo = sb("bo", [128, D])
        top = sb("top", [128, 2, H])
        rec = sb("rec", [128, 2, H])
        bn = sb("bn", [128, 6])
        mv = sb("mv", [128, 2, 2])
        ve = sb("ve", [128, 4])
        rstd = sb("rstd", [128, 2])
        half = sb("half", [128, 4])
        ident = sb("ident", [128, 128])
        w1_hi = sb("w1_hi", [128, FP], R)
        w1_lo = sb("w1_lo", [128, FP], R)
        w3_hi = sb("w3_hi", [128, FP], R)
        w3_lo = sb("w3_lo", [128, FP], R)
        rw = sb("rw", [128, E])
        rw_hi = sb("rw_hi", [128, E], R)
        rw_lo = sb("rw_lo", [128, E], R)
        sel = sb("sel", [128, FP], BF)
        amax = sb("amax", [128, 2])
        amall = sb("amall", [128, 2])
        sc = sb("sc", [128, 8])
        rank = sb("rank", [128, GB, E])

        wq_raw = O[0:DH, :, :].rearrange("p a n -> p (a n)")
        wk_raw = OT[0:DH, :, :, :].rearrange("p a c n -> p (a c n)")
        P_flat = P[:, :, :].rearrange("p a n -> p (a n)")
        wv_raw, wo_raw = P_flat[0:DC, 0:H * DH], P_flat[:, H * DH:2 * H * DH]
        w1_raw = pt_hi[:, :, :].rearrange("p a n -> p (a n)").bitcast(F)
        w3_raw = pt_lo[:, :, :].rearrange("p a n -> p (a n)").bitcast(F)
        G_flat = G[:, :, :, :].rearrange("p b h k -> p (b h k)")
        NF = NB * NK * DC // 128
        flat = G_flat[:, GB * HK:GB * HK + NF]
        w2 = P_flat[:, 0:FP].rearrange("p (c n) -> p c n", c=FC)
        NT = GB * NQ
        hid = G_flat[:, 0:FC * NT].rearrange("p (c n) -> p c n", c=FC)
        silu = G_flat[:, FC * NT:FC * NT + 2 * NT].rearrange("p (c n) -> p c n", c=2)
        gated = G_flat[:, (FC + 2) * NT:(FC + 4) * NT].rearrange("p (c n) -> p c n", c=2)
        x2T_hi, x2T_lo = a_hi, a_lo
        y2 = O[:, :, :].rearrange("p a n -> p (a n)")
        x2 = y2[:, 0:NT].rearrange("p (b n) -> p b n", b=GB)
        lgT = y2[0:E, NT:2 * NT]
        small = y2[:, 2 * NT:4 * NT]
        gate_rows = OT[:, 0, :, :].rearrange("p c n -> p (c n)")[:, 0:GB * 128]\
            .rearrange("p (b n) -> p b n", b=GB)
        gT = sb("gT", [128, 2 * NT], BF)

        SB = [bank(f"S{p}") for p in range(3)]
        QB = [bank(f"Q{p}") for p in range(2)]
        WB = [bank(f"W{p}") for p in range(3)]

        names = ("ld_x0 ld_x1 ld_x2 ld_ctx ld_ctx_rest ld_flat ld_qk ld_wv ld_wo ld_w1 ld_w3 ld_rw ld_id ld_sel ld_w2 ld_bo "
                 "ld_rank st_out amax_done amax_all scale_step wv_lo_done wo_done a_mm a_hi_done a_lo_done wv_hi_done "
                 "w1_hi_done w3_hi_done rw_hi_done w_lo_done half_set ones_set pt_zero "
                 "s_S s_V s_G s_O s_PT s_T s_out s_xT "
                 "a_G a_Vhi a_exp a_PThi a_T a_xT a_cg a_cv "
                 "d_max d_sub d_Vlo d_rec d_On d_PTlo d_res d_bn d_aggr d_xln d_cg d_cv p_ve p_rstd p_xb "
                 "b_x2T b_lgT b_lg b_gT b_a b_b b_g b_y "
                 "c_x2hi c_lgT c_gT c_silu v_x2lo v_bn v_aggr v_x2 v_gate v_step v_gated v_hid v_out q_rstd q_ve gt_zero").split()
        s = {n: sem(n) for n in names}

        FIRST, LOOP0, LOOP1, LAST = -GB, GB, NB - 2 * GB, NB + 1
        def on(t, lo, hi):
            return not isinstance(t, int) or lo <= t < hi

        def at_slot(t, *which):
            return isinstance(t, int) and t in which

        def wait(eng, name, value):
            if not isinstance(value, int) or value > 0:
                eng.wait_ge(s[name], value)

        def apart(eng):
            eng.nop(nofuse=True)

        def slots(eng, slot):
            for t in range(FIRST, LOOP0):
                slot(t, t % GB)
            with eng.Fori(1, LOOP1 // GB) as g:
                for j in range(GB):
                    slot(g * GB + j, j)
            for t in range(LOOP1, LAST + 1):
                slot(t, t % GB)

        def q_bank(j, c):
            return (5 * j + (0, 1, 3, 4)[c]) % 2

        def x_bank(j):
            return (5 * j + 2) % 2

        block = stack.enter_context(nc.Block())

        @block.sync
        def _(sp):
            sp.dma_start(wk_raw[:, 0:H * DC], wk_d).then_inc(s["ld_qk"], 16)
            sp.dma_start(wq_raw, wq_d).then_inc(s["ld_qk"], 16)
            sp.dma_start(ctx_raw[:, 0:GB * NK], ctx_d[:, 0:GB * NK]).then_inc(s["ld_ctx"], 16)
            sp.dma_start(ident[:, :], ident_d).then_inc(s["ld_id"], 16)
            sp.dma_start(X[:, 0:GB, :], x_d[:, 0:GB, :]).then_inc(s["ld_x0"], 16)
            sp.dma_start(flat, ctxflat_d).then_inc(s["ld_flat"], 16)
            sp.dma_start(wv_raw, wv_d).then_inc(s["ld_wv"], 16)
            sp.dma_start(wo_raw, wo_d).then_inc(s["ld_wo"], 16)
            sp.dma_start(bo[:, :], bo_d).then_inc(s["ld_bo"], 16)
            sp.dma_start(ctx_raw[:, GB * NK:], ctx_d[:, GB * NK:]).then_inc(s["ld_ctx_rest"], 16)
            sp.dma_start(w1_raw[:, 0:FP], w1_d).then_inc(s["ld_w1"], 16)
            sp.dma_start(w3_raw[:, 0:FP], w3_d).then_inc(s["ld_w3"], 16)
            sp.dma_start(rw[:, :], rw_d).then_inc(s["ld_rw"], 16)
            sp.dma_start(rank[:, :, :], rank_d).then_inc(s["ld_rank"], 16)
            sp.dma_start(X[:, GB:2 * GB, :], x_d[:, GB:2 * GB, :]).then_inc(s["ld_x1"], 16)
            sp.dma_start(X[:, 2 * GB:, :], x_d[:, 2 * GB:, :]).then_inc(s["ld_x2"], 16)
            sp.wait_ge(s["s_PT"], 4 * NB)
            sp.dma_start(w2, w2_d).then_inc(s["ld_w2"], 16)
            with sp.Fori(0, NG) as g:
                sp.wait_ge(s["v_out"], g + 1)
                sp.dma_start(out_d[:, ds(g * GB, GB), :], X[:, ds(g * GB, GB), :]).then_inc(s["st_out"], 16)
            sp.wait_ge(s["st_out"], 16 * NG)

        @block.gpsimd
        def _(pool):
            pool.dma_start(sel[:, :], sel_d).then_inc(s["ld_sel"], 16)
            pool.memset(half[:, :], -0.5).then_inc(s["half_set"], 1)
            for c in range(2):
                pool.wait_ge(s["amax_done"], c + 1)
                nc.gpsimd.partition_all_reduce(amall[:, c:c + 1], amax[:, c:c + 1], 128,
                                               bass.bass_isa.ReduceOp.max).then_inc(s["amax_all"], 1)
            pool.wait_ge(s["ld_bo"], 16)
            pool.wait_ge(s["half_set"], 1)

            def slot(t, j):
                if on(t, -2, NB - 2):
                    wait(pool, "d_aggr", t + 3)
                    apart(pool)
                    pool.tensor_scalar(ve[:, 0:1], mv[:, j % 2, 1:2], EPS, 1.0, ALU.add, ALU.mult).then_inc(s["p_ve"], 1)
                    pool.wait_ge(s["p_ve"], t + 3)
                    pool.tensor_tensor(rstd[:, j % 2:j % 2 + 1], ve[:, 0:1], half[:, 0:1], ALU.pow).then_inc(s["p_rstd"], 1)
                if on(t, 1, NB + 1):
                    if isinstance(t, int):
                        pool.wait_ge(s[("ld_x0", "ld_x1", "ld_x2")[min((t - 1) // GB, 2)]], 16)
                    if at_slot(t, LOOP0 - 1):
                        pool.wait_ge(s["ld_x2"], 16)
                    wait(pool, "d_res", t - 2)
                    k = (j + 1) % 2
                    pool.tensor_tensor(xb[:, k:k + 1, :], X[:, ds(t - 1, 1), :], bo[:, :].rearrange("p (a n) -> p a n", a=1),
                                       ALU.add).then_inc(s["p_xb"], 1)
            slots(pool, slot)

            with pool.Fori(0, NG) as g:
                pool.wait_ge(s["v_aggr"], g + 1)
                apart(pool)
                pool.tensor_scalar(ve[:, 0:4], small[:, 1:2 * GB:2], EPS, 1.0, ALU.add, ALU.mult).then_inc(s["q_ve"], 1)
                pool.wait_ge(s["q_ve"], g + 1)
                pool.tensor_tensor(small[:, 8:8 + GB], ve[:, 0:4], half[:, :], ALU.pow).then_inc(s["q_rstd"], 1)

        @block.scalar
        def _(act):
            for q in range(4):
                act.wait_ge(s["a_mm"], q + 1)
                act.activation(a_hi[0:DC, q * 512:(q + 1) * 512], [*SB, QB[0]][q][0:DC, :], ACT.Copy,
                               scale=DH ** -0.5).then_inc(s["a_hi_done"], 1)

            def slot(t, j):
                def context_high(t):
                    if isinstance(t, int):
                        act.wait_ge(s["ld_ctx" if t == FIRST else "ld_ctx_rest"], 16)
                    wait(act, "s_G", 4 * (t + 4))
                    apart(act)
                    act.activation(cg_hi[:, :], ctx_raw[:, ds((t + 4) * NK, GB * NK)], ACT.Copy).then_inc(s["a_cg"], 1)

                if at_slot(t, FIRST):
                    context_high(t)
                if on(t, -1, NB - 1):
                    wait(act, "s_V", 2 * t)
                    apart(act)
                    act.activation(cv_hi[:, (j + 1) % 2, :], ctx_raw[:, ds((t + 1) * NK, NK)], ACT.Copy).then_inc(s["a_cv"], 1)

                def v_high(k):
                    wait(act, "s_V", 2 * t + k + 1)
                    if k == 0:
                        wait(act, "s_O", 3 * (t - 1))
                    act.activation(v_hi[0:NK, j % 2, 8 * k:8 * k + 8, 0:DH],
                                   WB[k][0:NK, :].rearrange("p (h n) -> p h n", h=8), ACT.Copy).then_inc(s["a_Vhi"], 1)

                def exps(p):
                    lo, hi = SP[p]
                    wait(act, "d_sub", 3 * t + p + 1)
                    act.activation(P[:, j % 2, lo * NK:hi * NK], P[:, j % 2, lo * NK:hi * NK], ACT.Exp).then_inc(s["a_exp"], 1)

                def g_out(k):
                    wait(act, "s_G", 4 * (t + 4) + k + 1)
                    if k == 0 and j == 0:
                        wait(act, "s_S", 3 * t)
                    half_ = (t // GB + 1) % 2 if isinstance(t, int) else ((t + 4) // GB) % 2
                    apart(act)
                    act.activation(G[:, ds(half_ * GB, GB), 4 * j + k, :],
                                   WB[(2, 0, 1, 0)[k]][:, 0:GB * NK].rearrange("p (b n) -> p b n", b=GB),
                                   ACT.Copy).then_inc(s["a_G"], 1)

                def pt_high(c):
                    wait(act, "s_PT", 4 * t + c + 1)
                    if c == 0:
                        wait(act, "s_O", 3 * (t - 1))
                        if at_slot(t, 0, 1):
                            act.wait_ge(s["pt_zero"], 1)
                    act.activation(pt_hi[0:NK, j % 2, c * 512:(c + 1) * 512], QB[q_bank(j, c)][0:NK, :],
                                   ACT.Copy).then_inc(s["a_PThi"], 1)

                def oT(k):
                    wait(act, "s_T", 2 * (t - 1) + k + 1)
                    wait(act, "s_out", t - 2)
                    act.activation(OT[:, (j + 1) % 2, 4 * k:4 * k + 4, :],
                                   WB[1 + k][:, :].rearrange("p (c n) -> p c n", c=4), ACT.Copy).then_inc(s["a_T"], 1)

                now, gon, old = on(t, 0, NB), on(t, FIRST, NB - GB), on(t, 1, NB + 1)
                if now:
                    v_high(0); v_high(1); exps(0); exps(1)
                if gon:
                    g_out(0)
                if now:
                    exps(2)
                if now:
                    pt_high(0)
                if gon:
                    g_out(1)
                if now:
                    pt_high(1)
                if gon:
                    g_out(2)
                if on(t, -1, NB - 1):
                    wait(act, "s_xT", t + 2)
                    wait(act, "s_S", 3 * t)
                    act.activation(xT[:, (j + 1) % 2, :], QB[x_bank(j)][:, 0:NQ], ACT.Copy).then_inc(s["a_xT"], 1)
                if gon:
                    g_out(3)
                if on(t + 1, FIRST, NB - GB) and j == GB - 1:
                    context_high(t + 1)
                if old:
                    oT(0); oT(1)
                if now:
                    pt_high(2); pt_high(3)
                if at_slot(t, FIRST):
                    act.wait_ge(s["scale_step"], 6)
                    act.wait_ge(s["ld_wv"], 16)
                    act.activation(wv_hi[:, :], wv_raw, ACT.Copy, scale=sc[0:DC, 4:5]).then_inc(s["wv_hi_done"], 1)
                    act.wait_ge(s["ld_wo"], 16)
                    act.activation(wo[:, :, :], wo_raw.rearrange("p (c n) -> p c n", c=8), ACT.Copy,
                                   scale=sc[:, 5:6]).then_inc(s["wo_done"], 1)
                    for w, (hi, raw) in {"w1": (w1_hi, w1_raw), "w3": (w3_hi, w3_raw)}.items():
                        act.wait_ge(s["ld_" + w], 16)
                        act.activation(hi[:, :], raw[:, 0:FP], ACT.Copy).then_inc(s[w + "_hi_done"], 1)
                    act.wait_ge(s["ld_rw"], 16)
                    act.activation(rw_hi[:, :], rw[:, :], ACT.Copy).then_inc(s["rw_hi_done"], 1)
            slots(act, slot)

            def x2_high(g):
                act.wait_ge(s["b_x2T"], g + 1)
                wait(act, "b_b", FC * (g - 1))
                apart(act)
                act.activation(x2T_hi[:, ds(g % 2 * NT, NT)], QB[1][:, :], ACT.Copy).then_inc(s["c_x2hi"], 1)

            def logits_out(g):
                act.wait_ge(s["b_lgT"], g + 1)
                act.activation(lgT, QB[1][0:E, :], ACT.Copy).then_inc(s["c_lgT"], 1)

            def gates_out(g):
                act.wait_ge(s["b_gT"], g + 1)
                apart(act)
                act.activation(gT[:, ds(g % 2 * NT, NT)], QB[1][:, :], ACT.Copy).then_inc(s["c_gT"], 1)

            def chunk(g, c):
                act.wait_ge(s["b_a"], FC * g + c + 1)
                wait(act, "v_gated", FC * g + max(c - 1, 0))
                act.activation(silu[:, c % 2, :], SB[c % 2][:, :], ACT.Silu).then_inc(s["c_silu"], 1)

            def group(g, more):
                for c in range(FC):
                    chunk(g, c)
                    if more and c == 4:
                        x2_high(g + 1)
                    if more and c == 6:
                        logits_out(g + 1)
                    if more and c == 12:
                        gates_out(g + 1)

            act.wait_ge(s["s_S"], 3 * NB)
            x2_high(0)
            logits_out(0)
            gates_out(0)
            group(0, True)
            with act.Fori(1, NG - 1) as g:
                group(g, True)
            group(NG - 1, False)

        @block.vector
        def _(dve):
            dve.wait_ge(s["ld_flat"], 16)
            dve.tensor_reduce(amax[:, 0:1], flat, AX.X, ALU.max, apply_absolute_value=True).then_inc(s["amax_done"], 1)
            dve.memset(amax[:, 1:2], 0.0).then_inc(s["scale_step"], 1)
            dve.wait_ge(s["scale_step"], 1)
            dve.wait_ge(s["ld_wv"], 16)
            dve.tensor_reduce(amax[0:DC, 1:2], wv_raw, AX.X, ALU.max, apply_absolute_value=True).then_inc(s["amax_done"], 1)
            for q in range(4):
                dve.wait_ge(s["a_hi_done"], q + 1)
                dve.scalar_tensor_tensor(a_lo[0:DC, q * 512:(q + 1) * 512], [*SB, QB[0]][q][0:DC, :], DH ** -0.5,
                                         a_hi[0:DC, q * 512:(q + 1) * 512].bitcast(F), ALU.mult,
                                         ALU.subtract).then_inc(s["a_lo_done"], 1)
            dve.wait_ge(s["amax_all"], 2)
            dve.tensor_scalar(sc[:, 0:2], amall[:, :], TINY, None, ALU.max).then_inc(s["scale_step"], 1)
            dve.wait_ge(s["scale_step"], 2)
            dve.tensor_scalar(sc[:, 2:4].bitcast(U), sc[:, 0:2].bitcast(U), 0x7F800000, None,
                              ALU.bitwise_and).then_inc(s["scale_step"], 1)
            dve.wait_ge(s["scale_step"], 3)
            dve.tensor_scalar(sc[:, 5:6], sc[:, 2:3], sc[:, 3:4], 1.0 / VBOOST, ALU.mult, ALU.mult).then_inc(s["scale_step"], 1)
            dve.reciprocal(sc[:, 6:8], sc[:, 2:4]).then_inc(s["scale_step"], 1)
            dve.wait_ge(s["scale_step"], 5)
            dve.tensor_scalar(sc[:, 4:5], sc[:, 6:7], sc[:, 7:8], VBOOST, ALU.mult, ALU.mult).then_inc(s["scale_step"], 1)
            dve.memset(v_lo[:, :, :, :], 0.0).then_inc(s["ones_set"], 1)
            dve.memset(v_hi[:, :, :, :], 1.0).then_inc(s["ones_set"], 1)

            def slot(t, j):
                def context_low(t):
                    wait(dve, "a_cg", (t + 8) // GB)
                    dve.tensor_tensor(cg_lo[:, :], ctx_raw[:, ds((t + 4) * NK, GB * NK)], cg_hi[:, :].bitcast(F),
                                      ALU.subtract).then_inc(s["d_cg"], 1)

                if at_slot(t, FIRST):
                    context_low(t)

                def piece_max(p):
                    lo, hi = SP[p]
                    wait(dve, "s_S", 3 * t + p + 1)
                    dve.tensor_reduce(top[:, j % 2, lo:hi], SB[p][:, 0:(hi - lo) * NK].rearrange("p (h k) -> p h k", k=NK),
                                      AX.X, ALU.max).then_inc(s["d_max"], 1)

                def piece_sub(p):
                    lo, hi = SP[p]
                    wait(dve, "d_max", 3 * t + p + 1)
                    if p == 0:
                        wait(dve, "s_PT", 4 * (t - 1))
                        if at_slot(t, 0, 1):
                            dve.wait_ge(s["wv_lo_done"], 1)
                            dve.wait_ge(s["wo_done"], 1)
                    dve.tensor_tensor(P[:, j % 2, lo * NK:hi * NK].rearrange("p (h k) -> p h k", k=NK),
                                      SB[p][:, 0:(hi - lo) * NK].rearrange("p (h k) -> p h k", k=NK),
                                      top[:, j % 2, lo:hi].unsqueeze(2).broadcast_to([128, hi - lo, NK]),
                                      ALU.subtract).then_inc(s["d_sub"], 1)

                def v_low(k):
                    wait(dve, "a_Vhi", 2 * t + k + 1)
                    dve.tensor_tensor(v_lo[0:NK, j % 2, 8 * k:8 * k + 8, 0:DH],
                                      WB[k][0:NK, :].rearrange("p (h n) -> p h n", h=8),
                                      v_hi[0:NK, j % 2, 8 * k:8 * k + 8, 0:DH], ALU.subtract).then_inc(s["d_Vlo"], 1)

                def piece(p):
                    lo, hi = OP[p]
                    return SB[p][:, 0:(hi - lo) * (DH + 1)].rearrange("p (h n) -> p h n", n=DH + 1)

                def sums(p):
                    lo, hi = OP[p]
                    wait(dve, "s_O", 3 * (t - 1) + p + 1)
                    dve.reciprocal(rec[:, (j + 1) % 2, lo:hi].unsqueeze(2), piece(p)[:, :, DH:DH + 1]).then_inc(s["d_rec"], 1)

                def normed(p):
                    lo, hi = OP[p]
                    wait(dve, "d_rec", 3 * (t - 1) + p + 1)
                    wait(dve, "s_T", 2 * (t - 2))
                    dve.tensor_tensor(O[:, (j + 1) % 2, lo * DH:hi * DH].rearrange("p (h n) -> p h n", n=DH),
                                      piece(p)[:, :, 0:DH],
                                      rec[:, (j + 1) % 2, lo:hi].unsqueeze(2).broadcast_to([128, hi - lo, DH]),
                                      ALU.mult).then_inc(s["d_On"], 1)

                def pt_low(c):
                    wait(dve, "a_PThi", 4 * t + c + 1)
                    dve.tensor_tensor(pt_lo[0:NK, j % 2, c * 512:(c + 1) * 512], QB[q_bank(j, c)][0:NK, :],
                                      pt_hi[0:NK, j % 2, c * 512:(c + 1) * 512], ALU.subtract).then_inc(s["d_PTlo"], 1)

                if on(t, 0, NB):
                    piece_max(0); piece_max(1); piece_sub(0); piece_max(2); piece_sub(1); piece_sub(2)
                if on(t, -1, NB - 1):
                    wait(dve, "p_rstd", t + 2)
                    wait(dve, "s_xT", t)
                    k = (j + 1) % 2
                    dve.tensor_scalar(xln[:, k:k + 1, :], X[:, ds(t + 1, 1), :], mv[:, k, 0:1], rstd[:, k:k + 1],
                                      ALU.subtract, ALU.mult).then_inc(s["d_xln"], 1)
                if on(t, 0, NB):
                    v_low(0); v_low(1)
                if on(t, 1, NB + 1):
                    sums(0); sums(1); normed(0); sums(2); normed(1); normed(2)
                if on(t, 0, NB):
                    pt_low(0); pt_low(1)
                if on(t, 2, NB + 2):
                    wait(dve, "s_out", t - 1)
                    wait(dve, "p_xb", t - 1)
                    dve.tensor_tensor(X[:, ds(t - 2, 1), :], WB[2][:, 0:D].rearrange("p (a n) -> p a n", a=1),
                                      xb[:, j % 2:j % 2 + 1, :], ALU.add).then_inc(s["d_res"], 1)
                if on(t, -1, NB - 1):
                    wait(dve, "a_cv", t + 2)
                    dve.tensor_tensor(cv_lo[:, (j + 1) % 2, :], ctx_raw[:, ds((t + 1) * NK, NK)],
                                      cv_hi[:, (j + 1) % 2, :].bitcast(F), ALU.subtract).then_inc(s["d_cv"], 1)
                if on(t, -2, NB - 2):
                    if isinstance(t, int):
                        dve.wait_ge(s[("ld_x0", "ld_x1", "ld_x2")[min((t + 2) // GB, 2)]], 16)
                    if at_slot(t, LOOP0 - 1):
                        dve.wait_ge(s["ld_x2"], 16)
                    dve.bn_stats(bn[:, :], X[:, ds(t + 2, 1), :].rearrange("p a n -> p (a n)")).then_inc(s["d_bn"], 1)
                    dve.wait_ge(s["d_bn"], t + 3)
                    apart(dve)
                    dve.bn_aggr(mv[:, j % 2, :], bn[:, :]).then_inc(s["d_aggr"], 1)
                if on(t + 1, FIRST, NB - GB) and j == GB - 1:
                    context_low(t + 1)
                if on(t, 0, NB):
                    pt_low(2); pt_low(3)
                if at_slot(t, FIRST):
                    dve.wait_ge(s["wv_hi_done"], 1)
                    dve.scalar_tensor_tensor(wv_lo[:, :], wv_raw, sc[0:DC, 4:5], wv_hi[:, :].bitcast(F), ALU.mult,
                                             ALU.subtract).then_inc(s["wv_lo_done"], 1)
                    for w, hi, lo, raw in (("w1", w1_hi, w1_lo, w1_raw), ("w3", w3_hi, w3_lo, w3_raw)):
                        dve.wait_ge(s[w + "_hi_done"], 1)
                        dve.tensor_tensor(lo[:, :], raw[:, 0:FP], hi[:, :].bitcast(F), ALU.subtract).then_inc(s["w_lo_done"], 1)
                    dve.wait_ge(s["rw_hi_done"], 1)
                    dve.tensor_tensor(rw_lo[:, :], rw[:, :], rw_hi[:, :].bitcast(F), ALU.subtract).then_inc(s["w_lo_done"], 1)
                    dve.wait_ge(s["w_lo_done"], 3)
                    dve.memset(pt_hi[64:KR, :, :], 0.0)
                    dve.memset(pt_lo[64:KR, :, :], 0.0).then_inc(s["pt_zero"], 1)
            slots(dve, slot)

            steps = []

            def step(ins, g):
                ins.then_inc(s["v_step"], 1)
                steps.append(1)
                dve.wait_ge(s["v_step"], g * STEPS + len(steps))

            STEPS = 16

            def moments(g):
                for i in range(GB):
                    dve.bn_stats(small[:, 16 + 6 * i:22 + 6 * i],
                                 X[:, ds(g * GB + i, 1), :].rearrange("p a n -> p (a n)")).then_inc(s["v_bn"], 1)
                dve.wait_ge(s["v_bn"], GB * (g + 1))
                apart(dve)
                for i in range(GB):
                    last = dve.bn_aggr(small[:, 2 * i:2 * i + 2], small[:, 16 + 6 * i:22 + 6 * i])
                last.then_inc(s["v_aggr"], 1)

            def norm(g):
                wait(dve, "b_x2T", g)
                dve.wait_ge(s["v_aggr"], g + 1)
                dve.wait_ge(s["q_rstd"], g + 1)
                for i in range(GB):
                    last = dve.tensor_scalar(x2[:, i:i + 1, :], X[:, ds(g * GB + i, 1), :], small[:, 2 * i:2 * i + 1],
                                             small[:, 8 + i:9 + i], ALU.subtract, ALU.mult)
                last.then_inc(s["v_x2"], 1)

            def x2_low(g):
                dve.wait_ge(s["c_x2hi"], g + 1)
                dve.tensor_tensor(x2T_lo[:, ds(g % 2 * NT, NT)], QB[1][:, :], x2T_hi[:, ds(g % 2 * NT, NT)].bitcast(F),
                                  ALU.subtract).then_inc(s["v_x2lo"], 1)

            at = [64 + 32 * i for i in range(8)]
            tile = lambda n: small[:, at[n]:at[n] + GB * E].rearrange("p (b e) -> p b e", e=E)
            lg, eq, pick, pick2, rest, part, down = (tile(n) for n in range(7))
            bf = small[:, at[7]:at[7] + GB * E // 2].bitcast(BF).rearrange("p (b e) -> p b e", e=E)
            best, best_rank = small[:, 48:48 + GB], small[:, 52:52 + GB]
            hi, mid, lo = (gate_rows[:, :, GR * n:GR * n + E] for n in range(3))

            def wide(tiles):
                return tiles.unsqueeze(2).broadcast_to([128, GB, E])

            def largest(of, into, g):
                step(dve.tensor_reduce(best, of, AX.X, ALU.max), g)
                step(dve.tensor_tensor(eq, of, wide(best), ALU.is_equal), g)
                step(dve.tensor_tensor(eq, eq, rank[:, :, :], ALU.mult), g)
                step(dve.tensor_reduce(best_rank, eq, AX.X, ALU.max), g)
                step(dve.tensor_tensor(into, eq, wide(best_rank), ALU.is_equal), g)

            def gates_first(g):
                steps.clear()
                dve.wait_ge(s["b_lg"], g + 1)
                step(dve.tensor_copy(lg, QB[1][:, 0:GB * E].rearrange("p (b e) -> p b e", e=E)), g)
                largest(lg, pick, g)

            def gates_second(g):
                step(dve.scalar_tensor_tensor(rest, pick, -BIG, lg, ALU.mult, ALU.add), g)
                largest(rest, pick2, g)

            def gates_high(g):
                step(dve.tensor_tensor(pick, pick, pick2, ALU.add), g)
                step(dve.tensor_tensor(pick, pick, lg, ALU.mult), g)
                wait(dve, "b_gT", g)
                step(dve.tensor_copy(bf, pick), g)
                step(dve.tensor_copy(hi, bf), g)
                assert len(steps) == STEPS

            def gates_low(g):
                dve.tensor_tensor(part, pick, hi, ALU.subtract).then_inc(s["v_gate"], 1)
                dve.wait_ge(s["v_gate"], 5 * g + 1)
                dve.tensor_copy(bf, part).then_inc(s["v_gate"], 1)
                dve.wait_ge(s["v_gate"], 5 * g + 2)
                dve.tensor_copy(mid, bf).then_inc(s["v_gate"], 1)
                dve.wait_ge(s["v_gate"], 5 * g + 3)
                dve.tensor_tensor(down, part, mid, ALU.subtract).then_inc(s["v_gate"], 1)
                dve.wait_ge(s["v_gate"], 5 * g + 4)
                dve.tensor_copy(lo, down).then_inc(s["v_gate"], 1)

            def chunk(g, c):
                dve.wait_ge(s["c_silu"], FC * g + c + 1)
                dve.wait_ge(s["b_g"], FC * g + c + 1)
                wait(dve, "v_hid", FC * g + max(c - 1, 0))
                dve.tensor_tensor(gated[:, c % 2, :], WB[c % 2][:, :], silu[:, c % 2, :], ALU.mult).then_inc(s["v_gated"], 1)
                dve.wait_ge(s["v_gated"], FC * g + c + 1)
                dve.wait_ge(s["b_b"], FC * g + c + 1)
                wait(dve, "b_y", FC * (g - 1) + c + 1)
                dve.tensor_tensor(hid[:, c, :], (SB[2], QB[0])[c % 2][:, :], gated[:, c % 2, :], ALU.mult).then_inc(s["v_hid"], 1)

            def group(g, more):
                for c in range(FC):
                    chunk(g, c)
                    if c == 1 and (not isinstance(g, int) or g > 0):
                        result(g - 1)
                    if more and c == 2:
                        moments(g + 1)
                    if more and c == 3:
                        norm(g + 1)
                    if more and c == 4:
                        x2_low(g + 1)
                    if more and c == 7:
                        gates_first(g + 1)
                    if more and c == 8:
                        gates_second(g + 1)
                    if more and c == 9:
                        gates_high(g + 1)
                    if more and c == 10:
                        gates_low(g + 1)

            def result(g):
                dve.wait_ge(s["b_y"], FC * (g + 1))
                dve.tensor_tensor(X[:, ds(g * GB, GB), :], WB[2][:, :].rearrange("p (b n) -> p b n", b=GB),
                                  X[:, ds(g * GB, GB), :], ALU.add).then_inc(s["v_out"], 1)

            dve.wait_ge(s["s_out"], NB)
            dve.memset(gate_rows, 0.0).then_inc(s["gt_zero"], 1)
            dve.wait_ge(s["gt_zero"], 1)
            dve.memset(gate_rows[:, :, E:E + 1], 1.0).then_inc(s["gt_zero"], 1)
            dve.wait_ge(s["ld_rank"], 16)
            dve.wait_ge(s["d_res"], NB)
            moments(0)
            norm(0)
            x2_low(0)
            dve.wait_ge(s["gt_zero"], 2)
            gates_first(0)
            gates_second(0)
            gates_high(0)
            gates_low(0)
            group(0, True)
            with dve.Fori(1, NG - 1) as g:
                group(g, True)
            group(NG - 1, False)
            result(NG - 1)

        @block.tensor
        def _(pe):
            pe.wait_ge(s["ld_qk"], 32)
            for q in range(4):
                for i in range(4):
                    h = 4 * q + i
                    last = pe.matmul([*SB, QB[0]][q][0:DC, i * D:(i + 1) * D], wk_raw[:, h * DC:(h + 1) * DC],
                                     wq_raw[:, h * D:(h + 1) * D], start=True, stop=True)
                last.then_inc(s["a_mm"], 1)
            pe.wait_ge(s["a_lo_done"], 4)
            pe.wait_ge(s["ld_id"], 16)

            def three(out, w_hi, w_lo, m_hi, m_lo):
                pe.matmul(out, w_hi, m_hi, start=True, stop=False)
                pe.matmul(out, w_hi, m_lo, start=False, stop=False)
                return pe.matmul(out, w_lo, m_hi, start=False, stop=True)

            def slot(t, j):
                def scores():
                    wait(pe, "a_xT", t + 1)
                    wait(pe, "a_G", 4 * (t - j) + 16)
                    half_ = (t // GB) % 2 if isinstance(t, int) else (t // GB) % 2
                    for p, (lo, hi) in enumerate(SP):
                        wait(pe, "d_On", 3 * (t - 2) + p + 1)
                        pe.matmul(SB[p][:, 0:(hi - lo) * NK], xT[:, j % 2, :],
                                  G_flat[:, ds((half_ * GB + j) * HK + lo * NK, (hi - lo) * NK)],
                                  start=True, stop=True).then_inc(s["s_S"], 1)

                def values(k):
                    wait(pe, "d_cv", t + 1)
                    if k == 0:
                        wait(pe, "a_G", 4 * (t + 4) if on(t, FIRST, NB - GB) else 4 * (NB - GB))
                    else:
                        wait(pe, "a_T", 2 * (t - 2) + 1)
                    if at_slot(t, 0):
                        pe.wait_ge(s["wv_lo_done"], 1)
                        pe.wait_ge(s["a_G"], 16)
                    cols = slice(k * 512, (k + 1) * 512)
                    three(WB[k][0:NK, :], cv_hi[:, j % 2, :], cv_lo[:, j % 2, :], wv_hi[:, cols],
                          wv_lo[:, cols]).then_inc(s["s_V"], 1)

                def g_piece(k):
                    if k == 0:
                        wait(pe, "d_cg", (t + 8) // GB)
                        wait(pe, "a_T", 2 * (t - 2) + 2)
                        wait(pe, "a_G", 4 * (t + 4))
                    elif k < 3:
                        if on(t, 0, NB):
                            wait(pe, "d_Vlo", 2 * t + k)
                    else:
                        wait(pe, "a_G", 4 * (t + 4) + 2)
                    h = 4 * j + k
                    three(WB[(2, 0, 1, 0)[k]][:, 0:GB * NK], a_hi[0:DC, h * D:(h + 1) * D], a_lo[0:DC, h * D:(h + 1) * D],
                          cg_hi[:, :], cg_lo[:, :]).then_inc(s["s_G"], 1)

                def pv(p):
                    lo, hi = OP[p]
                    b = (j + 1) % 2
                    if on(t, 0, NB):
                        wait(pe, "d_sub", 3 * t + p + 1)
                    else:
                        wait(pe, "d_On", 3 * (t - 2) + p + 1)
                    if p == 0:
                        wait(pe, "d_PTlo", 4 * t)
                        wait(pe, "d_Vlo", 2 * t)
                        if at_slot(t, 1):
                            pe.wait_ge(s["ones_set"], 2)
                    for i, h in enumerate(range(lo, hi)):
                        out = SB[p][:, i * (DH + 1):(i + 1) * (DH + 1)]
                        ph, pl = (w[0:KR, b, h * NQ:(h + 1) * NQ] for w in (pt_hi, pt_lo))
                        pe.matmul(out, ph, v_hi[:, b, h, :], start=True, stop=False)
                        pe.matmul(out, ph, v_lo[:, b, h, :], start=False, stop=False)
                        last = pe.matmul(out, pl, v_hi[:, b, h, :], start=False, stop=True)
                    last.then_inc(s["s_O"], 1)

                def p_turn(c):
                    wait(pe, "a_exp", 3 * t + (1, 2, 2, 3)[c])
                    if c < 3:
                        wait(pe, "d_PTlo", 4 * t + (-1, 0, 2)[c])
                    elif on(t, -1, NB - 1):
                        wait(pe, "a_xT", t + 2)
                    else:
                        wait(pe, "d_PTlo", 4 * t + 1)
                    for i in range(4):
                        h = 4 * c + i
                        last = pe.transpose(QB[q_bank(j, c)][0:NK, i * NQ:(i + 1) * NQ],
                                            P[:, j % 2, h * NK:(h + 1) * NK], ident[:, :])
                    last.then_inc(s["s_PT"], 1)

                def o_turn(k):
                    wait(pe, "d_On", 3 * (t - 1) + k + 2)
                    if k == 0:
                        if on(t, FIRST, NB - GB):
                            wait(pe, "a_G", 4 * (t + 4) + 3)
                        elif on(t, 0, NB):
                            wait(pe, "d_Vlo", 2 * t + 2)
                        else:
                            wait(pe, "a_T", 2 * (t - 2) + 1)
                    else:
                        wait(pe, "d_res", t - 1)
                    for i in range(4):
                        c = 4 * k + i
                        last = pe.transpose(WB[1 + k][:, i * NQ:(i + 1) * NQ], O[:, (j + 1) % 2, c * 128:(c + 1) * 128], ident[:, :])
                    last.then_inc(s["s_T"], 1)

                def project():
                    wait(pe, "a_T", 2 * (t - 1))
                    if on(t, FIRST, NB - GB):
                        wait(pe, "a_G", 4 * (t + 4) + 1)
                    if at_slot(t, 2):
                        pe.wait_ge(s["wo_done"], 1)
                    for c in range(8):
                        last = pe.matmul(WB[2][:, 0:D], OT[:, j % 2, c, :], wo[:, c, :], start=(c == 0), stop=(c == 7))
                    last.then_inc(s["s_out"], 1)

                now, gon, old = on(t, 0, NB), on(t, FIRST, NB - GB), on(t, 1, NB + 1)
                if now:
                    scores(); values(0); values(1)
                if gon:
                    g_piece(0)
                if old:
                    pv(0); pv(1); pv(2)
                if now:
                    p_turn(0)
                if gon:
                    g_piece(1)
                if now:
                    p_turn(1)
                if gon:
                    g_piece(2)
                if on(t, 2, NB + 2):
                    project()
                if on(t, -1, NB - 1):
                    wait(pe, "d_xln", t + 2)
                    wait(pe, "d_PTlo", 4 * t + 1)
                    pe.transpose(QB[x_bank(j)][:, 0:NQ], xln[:, (j + 1) % 2, :], ident[:, :]).then_inc(s["s_xT"], 1)
                if gon:
                    g_piece(3)
                if old:
                    o_turn(0); o_turn(1)
                if now:
                    p_turn(2); p_turn(3)
            slots(pe, slot)

            def x2_turn(g):
                pe.wait_ge(s["v_x2"], g + 1)
                wait(pe, "c_gT", g)
                for i in range(GB):
                    last = pe.transpose(QB[1][:, i * NQ:(i + 1) * NQ], x2[:, i, :], ident[:, :])
                last.then_inc(s["b_x2T"], 1)

            def logits(g):
                pe.wait_ge(s["v_x2lo"], g + 1)
                at = ds(g % 2 * NT, NT)
                three(QB[1][0:E, :], rw_hi[:, :], rw_lo[:, :], x2T_hi[:, at], x2T_lo[:, at]).then_inc(s["b_lgT"], 1)

            def logits_turn(g):
                pe.wait_ge(s["c_lgT"], g + 1)
                apart(pe)
                for i in range(GB):
                    last = pe.transpose(QB[1][:, i * E:(i + 1) * E], lgT[:, i * NQ:(i + 1) * NQ], ident[0:E, 0:E])
                last.then_inc(s["b_lg"], 1)

            def gates_turn(g):
                pe.wait_ge(s["v_gate"], 5 * g + 5)
                for i in range(GB):
                    last = pe.transpose(QB[1][:, i * NQ:(i + 1) * NQ], gate_rows[:, i, :], ident[:, :])
                last.then_inc(s["b_gT"], 1)

            def up(g, c):
                at, cols = ds(g % 2 * NT, NT), slice(c * 128, (c + 1) * 128)
                before = FC * g + max(c - 1, 0)
                wait(pe, "c_silu", before)
                three(SB[c % 2][:, :], w1_hi[:, cols], w1_lo[:, cols], x2T_hi[:, at], x2T_lo[:, at]).then_inc(s["b_a"], 1)
                if c == 0:
                    pe.wait_ge(s["c_gT"], g + 1)
                wait(pe, "v_gated", before)
                pe.matmul(WB[c % 2][:, :], sel[:, cols], gT[:, at], start=True, stop=True).then_inc(s["b_g"], 1)
                wait(pe, "v_hid", before)
                three((SB[2], QB[0])[c % 2][:, :], w3_hi[:, cols], w3_lo[:, cols], x2T_hi[:, at], x2T_lo[:, at]).then_inc(s["b_b"], 1)

            def down(g, c):
                pe.wait_ge(s["v_hid"], FC * g + c + 1)
                if c == 0:
                    wait(pe, "v_out", g)
                for i in range(GB):
                    last = pe.matmul(WB[2][:, i * D:(i + 1) * D], hid[:, c, i * NQ:(i + 1) * NQ], w2[:, c, :],
                                     start=(c == 0 and i == 0), stop=(c == FC - 1), skip_group_check=True)
                last.then_inc(s["b_y"], 1)

            def group(g, more):
                for c in range(FC):
                    up(g, c)
                    if c >= 2:
                        down(g, c - 2)
                    elif not isinstance(g, int) or g > 0:
                        down(g - 1, FC - 2 + c)
                    if more and c == 4:
                        x2_turn(g + 1)
                    if more and c == 6:
                        logits(g + 1)
                    if more and c == 7:
                        logits_turn(g + 1)
                    if more and c == 12:
                        gates_turn(g + 1)

            pe.wait_ge(s["w_lo_done"], 3)
            pe.wait_ge(s["ld_sel"], 16)
            pe.wait_ge(s["ld_w2"], 16)
            pe.wait_ge(s["d_PTlo"], 4 * NB)
            pe.wait_ge(s["a_T"], 2 * NB)
            pe.wait_ge(s["d_On"], 3 * NB)
            pe.wait_ge(s["d_res"], NB)
            x2_turn(0)
            logits(0)
            logits_turn(0)
            gates_turn(0)
            group(0, True)
            with pe.Fori(1, NG - 1) as g:
                group(g, True)
            group(NG - 1, False)
            down(NG - 1, FC - 2)
            down(NG - 1, FC - 1)


def kernel(x, ctx_768, L0_xattn_w_q, L0_xattn_w_kv, L0_xattn_w_out, L0_xattn_b_out, L0_ffn_router_w,
           L0_ffn_w1, L0_ffn_w2, L0_ffn_w3, L0_ffn_sw1, L0_ffn_sw2, L0_ffn_sw3):
    import concourse.bacc as bacc
    from concourse.bass_utils import run_bass_kernel_spmd

    f = np.float32
    x, ctx = np.asarray(x), np.asarray(ctx_768)
    wq, wkv, wout, bout = (np.asarray(a) for a in (L0_xattn_w_q, L0_xattn_w_kv, L0_xattn_w_out, L0_xattn_b_out))
    w1, w2, w3 = (np.asarray(a) for a in (L0_ffn_w1, L0_ffn_w2, L0_ffn_w3))
    sw1, sw2, sw3 = (np.asarray(a) for a in (L0_ffn_sw1, L0_ffn_sw2, L0_ffn_sw3))
    inner = H * DH
    pad = np.zeros((FP - FU, D), f)
    sel = np.zeros((128, FP), f)
    for part in range(3):
        for e in range(E + 1):
            if e < E or part == 0:
                sel[part * GR + e, e * I:(e + 1) * I] = 1.0
    rank = np.broadcast_to(np.arange(E, 0, -1, dtype=f), (128, GB, E))
    arrays = {
        "x": x.transpose(1, 0, 2),
        "ctxT": ctx.transpose(2, 0, 1).reshape(DC, NB * NK),
        "ctx_flat": ctx.reshape(128, -1),
        "wqT": wq.reshape(D, H, DH).transpose(2, 1, 0).reshape(DH, H * D),
        "wkT": wkv[:, :inner].reshape(DC, H, DH).transpose(2, 1, 0).reshape(DH, H * DC),
        "wv": wkv[:, inner:],
        "wo": wout.reshape(8, 128, D).transpose(1, 0, 2).reshape(128, 8 * D),
        "bo": np.broadcast_to(bout, (128, D)),
        "rwT": np.asarray(L0_ffn_router_w).T,
        "w1T": np.concatenate([w1.reshape(E * I, D), sw1, pad]).T,
        "w3T": np.concatenate([w3.reshape(E * I, D), sw3, pad]).T,
        "w2": np.concatenate([w2.transpose(0, 2, 1).reshape(E * I, D), sw2.T, pad]).reshape(FC, 128, D).transpose(1, 0, 2),
        "sel": sel, "ident": np.eye(128, dtype=f), "rank": rank,
    }
    arrays = {n: np.ascontiguousarray(a) for n, a in arrays.items()}
    nc = bacc.Bacc("TRN2", target_bir_lowering=False, num_devices=1)
    ins = [nc.dram_tensor(n + "_in", a.shape, mybir.dt.from_np(a.dtype), kind="ExternalInput").ap() for n, a in arrays.items()]
    out = nc.dram_tensor("y_out", (128, NB, D), mybir.dt.float32, kind="ExternalOutput").ap()
    program(nc, *ins, out)
    got = run_bass_kernel_spmd(nc, [{n + "_in": a for n, a in arrays.items()}], core_ids=[0])
    return got.results[0]["y_out"].transpose(1, 0, 2)
```

```python
import numpy as np
import concourse.bass as bass
from concourse import mybir
from contextlib import ExitStack

NB, NQ, D = 64, 128, 128
NK, DC = 77, 96
H, DH = 16, 64
E, I = 8, 176
GB = 4
NG = NB // GB
HK = H * NK
KR = 96
FU = (E + 1) * I
FC = -(-FU // 128)
FP = FC * 128
FL = FU - (FC - 1) * 128
SP = [(0, 6), (6, 12), (12, 16)]
CP = [(0, GB), (GB, 34), (34, NB)]
OP = [(0, 6), (6, 11), (11, 16)]
GR = 16
EPS = 1e-5
VBOOST = 128.0
WBOOST = 16384.0
TINY = 2.0 ** -60
BIG = 3.0e38


def program(nc, x_d, ctx_d, wq_d, wk_d, wv_d, wo_d, bo_d, rw_d, w1_d, w3_d, w2_d, sel_d,
            ident_d, rank_d, out_d):
    F, R, HF, BF, U = (mybir.dt.float32, mybir.dt.float32r, mybir.dt.float16, mybir.dt.bfloat16,
                       mybir.dt.uint32)
    ACT, ALU, AX = mybir.ActivationFunctionType, mybir.AluOpType, mybir.AxisListType
    ds = bass.ds
    stack = ExitStack()
    with stack:
        def sb(name, shape, dt=F):
            return stack.enter_context(nc.sbuf_tensor(name, shape, dt))

        def bank(name):
            return stack.enter_context(nc.psum_tensor(name, [128, 512], F))

        def sem(name):
            return stack.enter_context(nc.semaphore(name))

        X = sb("X", [128, NB, D])
        ctx_rows = sb("ctx_raw", [128, NB * NK])
        a_hi = sb("a_hi", [128, H * D], R)
        a_lo = sb("a_lo", [128, H * D], R)
        wv_hi = sb("wv_hi", [DC, H * DH], R)
        wv_lo = sb("wv_lo", [DC, H * DH], R)
        wo_hi = sb("wo_hi", [128, 8, D], HF)
        wo_lo = sb("wo_lo", [128, 8, D], HF)
        cg_hi = sb("cg_hi", [DC, GB * NK], R)
        cg_lo = sb("cg_lo", [DC, GB * NK], R)
        cv_hi = sb("cv_hi", [DC, 2, NK], R)
        cv_lo = sb("cv_lo", [DC, 2, NK], R)
        xln = sb("xln", [128, 2, D])
        xT = sb("xT", [128, 2, NQ])
        P = sb("P", [128, 2, HK])
        v_hi = sb("v_hi", [KR, 2, H, DH + 1], HF)
        v_lo = sb("v_lo", [KR, 2, H, DH + 1], HF)
        O = sb("O", [128, 2, H * DH])
        OT = sb("OT", [128, 8, NQ])
        OT_hi = sb("OT_hi", [128, 8, NQ], HF)
        OT_lo = sb("OT_lo", [128, 8, NQ], HF)
        xb = sb("xb", [128, 2, D])
        bo = sb("bo", [128, D])
        top = sb("top", [128, 2, H])
        rec = sb("rec", [128, 2, H])
        bn = sb("bn", [128, 6])
        mv = sb("mv", [128, 2, 2])
        ve = sb("ve", [128, 1])
        rstd = sb("rstd", [128, 2])
        half = sb("half", [128, 4])
        ident = sb("ident", [128, 128])
        w1_hi = sb("w1_hi", [128, FP], R)
        w1_lo = sb("w1_lo", [128, FP], R)
        w3_hi = sb("w3_hi", [128, FP - 128], R)
        w3_lo = sb("w3_lo", [128, FP - 128], R)
        rw = sb("rw", [128, E])
        sel = sb("sel", [128, FP], BF)
        amax = sb("amax", [128, 4])
        amall = sb("amall", [128, 4])
        amax_o = sb("amax_o", [128, 2])
        sc = sb("sc", [128, 8])
        so = sb("so", [128, 5])
        rank = sb("rank", [128, GB, E])
        gT = sb("gT", [128, 2 * GB * NQ], BF)

        NT = GB * NQ
        LAG = 3
        HS, HP = 3, LAG
        with ExitStack() as phase_a:
            def early(name, shape, dt=F):
                return phase_a.enter_context(nc.sbuf_tensor(name, shape, dt))

            G = early("G", [128, 2 * GB, H, NK])
            pt_hi = early("pt_hi", [128, 2, H * NQ], HF)
            pt_lo = early("pt_lo", [128, 2, H * NQ], HF)
        silu = sb("silu", [128, 2, NT])
        gated = sb("gated", [128, 2, NT])
        hid = sb("hid", [128, HS + 1, NT])
        hid_hi = sb("hid_hi", [128, HP + 1, NT], R)
        hid_lo = sb("hid_lo", [128, HP + 1, NT], R)
        w2_hi = sb("w2_hi", [128, FP], R)
        w2_lo = sb("w2_lo", [128, FP], R)

        ctx_raw = ctx_rows[0:DC, :]
        wq_raw = O[0:DH, :, :].rearrange("p a n -> p (a n)")
        P_flat = P[:, :, :].rearrange("p a n -> p (a n)")
        wv_raw = P_flat[0:DC, 0:H * DH]
        X_flat = X[:, :, :].rearrange("p b n -> p (b n)")
        w1_raw = X_flat[:, 2 * GB * D:2 * GB * D + FP]
        w3_raw = X_flat[:, 2 * GB * D + FP:2 * GB * D + 2 * FP - 128]
        wo_raw = X_flat[:, 2 * GB * D + 2 * FP:2 * GB * D + 2 * FP + H * DH]
        wk_raw = X_flat[0:DH, 2 * GB * D + 2 * FP + H * DH:2 * GB * D + 2 * FP + H * DH + H * DC]
        G_flat = G[:, :, :, :].rearrange("p b h k -> p (b h k)")
        w2_raw = hid[:, :, :].rearrange("p c n -> p (c n)")[:, 0:FP]
        x2T_hi, x2T_lo = a_hi, a_lo
        x2 = ctx_rows[:, 0:NT].rearrange("p (b n) -> p b n", b=GB)
        gate_rows = ctx_rows[:, NT:2 * NT].rearrange("p (b n) -> p b n", b=GB)
        x2T = ctx_rows[:, 2 * NT:3 * NT]
        small = ctx_rows[:, 3 * NT:4 * NT]
        y_T = ctx_rows[:, 4 * NT:5 * NT]

        SB = [bank(f"S{p}") for p in range(3)]
        QB = [bank(f"Q{p}") for p in range(2)]
        WB = [bank(f"W{p}") for p in range(3)]

        names = ("ld_x0 ld_x1 ld_x2 ld_ctx0 ld_ctx1 ld_ctx2 ld_qk0 ld_qk1 ld_wv ld_wo ld_w1 ld_w3 ld_rw ld_id ld_sel "
                 "ld_w2 ld_bo ld_rank st_out amax_zero amax_done amax_all scale_step wv_lo_done amax_o_done amax_o_all wo_step "
                 "wo_hi_done wo_lo_done a_mm a_hi_done a_lo_done wv_hi_done "
                 "w1_hi_done w3_hi_done w2_hi_done w2_lo_done w_lo_done half_set ones_set pt_zero "
                 "s_S s_V s_G s_O s_PT s_T s_out s_xT "
                 "a_G a_Vhi a_exp a_PThi a_T a_xT a_cg a_cv "
                 "d_max d_sub d_Vlo d_rec d_On d_PTlo d_res d_bn d_aggr d_xln d_cg d_cv p_ve p_rstd p_xb "
                 "b_x2T b_lg b_gT b_a b_b b_g b_y b_yt "
                 "c_x2hi c_x2T c_gT c_silu c_hid c_yT r_hid r_x2lo "
                 "v_bn v_aggr v_x2 v_gate v_step v_gated v_hid v_out r_T q_rstd q_ve gt_zero").split()
        s = {n: sem(n) for n in names}

        FIRST, LOOP0, LOOP1, LAST = -GB, GB, NB - 2 * GB, NB + 1
        HEAD = NB - GB

        def on(t, lo, hi):
            return not isinstance(t, int) or lo <= t < hi

        def at_slot(t, *which):
            return isinstance(t, int) and t in which

        def wait(eng, name, value):
            if not isinstance(value, int) or value > 0:
                eng.wait_ge(s[name], value)

        def apart(eng):
            eng.nop(nofuse=True)

        def buffer(c, n):
            return c % n if c < FC - 1 else n

        def past(g, c, n):
            return FC * g + (0 if c == FC - 1 else c - n + (c >= n))

        def slots(eng, slot):
            for t in range(FIRST, LOOP0):
                slot(t, t % GB)
            with eng.Fori(1, LOOP1 // GB) as g:
                for j in range(GB):
                    slot(g * GB + j, j)
            for t in range(LOOP1, LAST + 1):
                slot(t, t % GB)

        def q_bank(j, c):
            return (5 * j + (0, 1, 3, 4)[c]) % 2

        def misc(g):
            return WB[0] if isinstance(g, int) and g == 0 else QB[1]

        def g_bank(t, k):
            if isinstance(t, int) and t < 0 and k == 3:
                return SB[(t - FIRST) % 3]
            return WB[(2, 0, 1, 0)[k]]

        def up_banks(c):
            if c == FC - 1:
                return SB[0], SB[0]
            if c == 0:
                return SB[2], SB[1]
            return SB[c % 2 if c > 2 else 0], (SB[2], QB[0])[c % 2]

        def x_bank(j):
            return (5 * j + 2) % 2

        block = stack.enter_context(nc.Block())

        @block.sync
        def _(sp):
            for k, (lo, hi) in enumerate(((0, 4), (4, H))):
                sp.dma_start(wk_raw[:, lo * DC:hi * DC], wk_d[:, lo * DC:hi * DC]).then_inc(s[f"ld_qk{k}"], 16)
                sp.dma_start(wq_raw[:, lo * D:hi * D], wq_d[:, lo * D:hi * D]).then_inc(s[f"ld_qk{k}"], 16)
            for k, (lo, hi) in enumerate(CP):
                sp.dma_start(ctx_raw[:, lo * NK:hi * NK], ctx_d[:, lo * NK:hi * NK]).then_inc(s[f"ld_ctx{k}"], 16)
                if k == 0:
                    sp.dma_start(wv_raw, wv_d).then_inc(s["ld_wv"], 16)
            sp.dma_start(X[:, 0:GB, :], x_d[:, 0:GB, :]).then_inc(s["ld_x0"], 16)
            sp.dma_start(ident[:, :], ident_d).then_inc(s["ld_id"], 16)
            sp.dma_start(bo[:, :], bo_d).then_inc(s["ld_bo"], 16)
            sp.dma_start(rw[:, :], rw_d).then_inc(s["ld_rw"], 16)
            sp.dma_start(wo_raw, wo_d).then_inc(s["ld_wo"], 16)
            sp.dma_start(X[:, GB:2 * GB, :], x_d[:, GB:2 * GB, :]).then_inc(s["ld_x1"], 16)
            sp.dma_start(w1_raw, w1_d).then_inc(s["ld_w1"], 16)
            sp.dma_start(w3_raw, w3_d).then_inc(s["ld_w3"], 16)
            sp.dma_start(rank[:, :, :], rank_d).then_inc(s["ld_rank"], 16)
            sp.wait_ge(s["w_lo_done"], 2)
            sp.wait_ge(s["wo_lo_done"], 1)
            sp.dma_start(X[:, 2 * GB:, :], x_d[:, 2 * GB:, :]).then_inc(s["ld_x2"], 16)
            sp.wait_ge(s["s_S"], 3 * HEAD)
            sp.dma_start(w2_raw, w2_d).then_inc(s["ld_w2"], 16)
            with sp.Fori(0, NG) as g:
                sp.wait_ge(s["v_out"], g + 1)
                sp.dma_start(out_d[:, ds(g * GB, GB), :], X[:, ds(g * GB, GB), :]).then_inc(s["st_out"], 16)
            sp.wait_ge(s["st_out"], 16 * NG)

        @block.gpsimd
        def _(pool):
            pool.dma_start(sel[:, :], sel_d).then_inc(s["ld_sel"], 16)
            pool.memset(half[:, :], -0.5).then_inc(s["half_set"], 1)
            pool.memset(amax[:, :], 0.0).then_inc(s["amax_zero"], 1)
            pool.memset(v_lo[:, :, :, :], 0.0).then_inc(s["ones_set"], 1)
            pool.memset(v_hi[:, :, :, :], 1.0).then_inc(s["ones_set"], 1)
            pool.wait_ge(s["ones_set"], 2)
            for pt in (pt_hi, pt_lo):
                pool.memset(pt[64:KR, :, :].rearrange("p a n -> p (a n)").bitcast(F), 0.0).then_inc(s["pt_zero"], 1)
            pool.wait_ge(s["pt_zero"], 2)
            pool.wait_ge(s["amax_done"], 4)
            nc.gpsimd.partition_all_reduce(amall[:, :], amax[:, :], 128, bass.bass_isa.ReduceOp.max).then_inc(s["amax_all"], 1)
            pool.wait_ge(s["half_set"], 1)

            def spread(g):
                pool.wait_ge(s["v_aggr"], g + 1)
                apart(pool)
                pool.tensor_scalar(small[:, 12:12 + GB], small[:, 1:2 * GB:2], EPS, 1.0, ALU.add, ALU.mult).then_inc(s["q_ve"], 1)
                pool.wait_ge(s["q_ve"], g + 1)
                pool.tensor_tensor(small[:, 8:8 + GB], small[:, 12:12 + GB], half[:, :], ALU.pow).then_inc(s["q_rstd"], 1)

            def x2_low(g):
                pool.wait_ge(s["c_x2hi"], g + 1)
                apart(pool)
                pool.tensor_tensor(x2T_lo[:, ds(g % 2 * NT, NT)], x2T, x2T_hi[:, ds(g % 2 * NT, NT)].bitcast(F),
                                   ALU.subtract).then_inc(s["r_x2lo"], 1)

            def slot(t, j):
                if on(t, -2, NB - 2):
                    wait(pool, "d_aggr", t + 3)
                    apart(pool)
                    pool.tensor_scalar(ve[:, 0:1], mv[:, j % 2, 1:2], EPS, 1.0, ALU.add, ALU.mult).then_inc(s["p_ve"], 1)
                    pool.wait_ge(s["p_ve"], t + 3)
                    pool.tensor_tensor(rstd[:, j % 2:j % 2 + 1], ve[:, 0:1], half[:, 0:1], ALU.pow).then_inc(s["p_rstd"], 1)
                if at_slot(t, 1):
                    pool.wait_ge(s["amax_o_done"], 1)
                    nc.gpsimd.partition_all_reduce(amax_o[:, 1:2], amax_o[:, 0:1], 128,
                                                   bass.bass_isa.ReduceOp.max).then_inc(s["amax_o_all"], 1)
                if on(t, 1, NB + 1):
                    if isinstance(t, int):
                        pool.wait_ge(s[("ld_x0", "ld_x1", "ld_x2")[min((t - 1) // GB, 2)]], 16)
                        if t == 1:
                            pool.wait_ge(s["ld_bo"], 16)
                    elif j == 1:
                        pool.wait_ge(s["ld_x2"], 16)
                    wait(pool, "d_res", t - 2)
                    k = (j + 1) % 2
                    pool.tensor_tensor(xb[:, k:k + 1, :], X[:, ds(t - 1, 1), :], bo[:, :].rearrange("p (a n) -> p a n", a=1),
                                       ALU.add).then_inc(s["p_xb"], 1)
                for k in range(2) if on(t, 1, NB + 1) else ():
                    wait(pool, "a_T", 2 * (t - 1) + k + 1)
                    half_ = slice(4 * k, 4 * k + 4)
                    pool.tensor_tensor(OT_lo[:, half_, :], OT[:, half_, :], OT_hi[:, half_, :],
                                       ALU.subtract).then_inc(s["r_T"], 1)
                if at_slot(t, 0, 1):
                    w, hi, lo, raw = (("w1", w1_hi, w1_lo, w1_raw), ("w3", w3_hi, w3_lo, w3_raw))[t]
                    pool.wait_ge(s[w + "_hi_done"], 1)
                    pool.tensor_tensor(lo[:, :], raw, hi[:, :].bitcast(F), ALU.subtract).then_inc(s["w_lo_done"], 1)
                if at_slot(t, HEAD):
                    spread(0)
                if at_slot(t, HEAD + 3):
                    x2_low(0)
            slots(pool, slot)

            def group(g, more):
                for c in range(FC):
                    pool.wait_ge(s["c_hid"], FC * g + c + 1)
                    k = buffer(c, HP)
                    pool.tensor_tensor(hid_lo[:, k, :], hid[:, buffer(c, HS), :], hid_hi[:, k, :].bitcast(F),
                                       ALU.subtract).then_inc(s["r_hid"], 1)
                    if more and c == 0:
                        spread(g + 1)
                    if more and c == 5:
                        x2_low(g + 1)
            group(0, True)
            with pool.Fori(1, NG - 1) as g:
                group(g, True)
            group(NG - 1, False)

        @block.scalar
        def _(act):
            def context_high(t):
                if isinstance(t, int):
                    act.wait_ge(s["ld_ctx0" if t == FIRST else "ld_ctx1"], 16)
                    if t == 0:
                        act.wait_ge(s["ld_ctx2"], 16)
                wait(act, "s_G", 4 * (t + 4))
                apart(act)
                act.activation(cg_hi[:, :], ctx_raw[:, ds((t + 4) * NK, GB * NK)], ACT.Copy).then_inc(s["a_cg"], 1)

            for q in range(4):
                act.wait_ge(s["a_mm"], q + 1)
                act.activation(a_hi[0:DC, q * 512:(q + 1) * 512], [*SB, QB[0]][q][0:DC, :], ACT.Copy,
                               scale=DH ** -0.5).then_inc(s["a_hi_done"], 1)
                if q == 1:
                    context_high(FIRST)

            def x2_high(g):
                wait(act, "b_lg", g)
                wait(act, "r_x2lo", g)
                act.wait_ge(s["b_x2T"], g + 1)
                act.activation(x2T, misc(g)[:, :], ACT.Copy).then_inc(s["c_x2T"], 1)
                wait(act, "b_a", FC * (g - 1))
                act.wait_ge(s["c_x2T"], g + 1)
                apart(act)
                act.activation(x2T_hi[:, ds(g % 2 * NT, NT)], x2T, ACT.Copy).then_inc(s["c_x2hi"], 1)

            def gates_out(g):
                act.wait_ge(s["b_gT"], g + 1)
                apart(act)
                act.activation(gT[:, ds(g % 2 * NT, NT)], misc(g)[:, :], ACT.Copy).then_inc(s["c_gT"], 1)

            def slot(t, j):
                if on(t, -1, NB - 1):
                    wait(act, "s_V", 2 * t)
                    apart(act)
                    act.activation(cv_hi[:, (j + 1) % 2, :], ctx_raw[:, ds((t + 1) * NK, NK)], ACT.Copy).then_inc(s["a_cv"], 1)

                def v_high(k):
                    wait(act, "s_V", 2 * t + k + 1)
                    if k == 0:
                        wait(act, "s_O", 3 * (t - 1))
                    act.activation(v_hi[0:NK, j % 2, 8 * k:8 * k + 8, 0:DH],
                                   WB[k][0:NK, :].rearrange("p (h n) -> p h n", h=8), ACT.Copy).then_inc(s["a_Vhi"], 1)

                def exps(p):
                    lo, hi = SP[p]
                    wait(act, "d_sub", 3 * t + p + 1)
                    act.activation(P[:, j % 2, lo * NK:hi * NK], P[:, j % 2, lo * NK:hi * NK], ACT.Exp).then_inc(s["a_exp"], 1)

                def g_out(k):
                    wait(act, "s_G", 4 * (t + 4) + k + 1)
                    if k == 0 and j == 0:
                        wait(act, "s_S", 3 * t)
                    half_ = (t // GB + 1) % 2 if isinstance(t, int) else ((t + 4) // GB) % 2
                    apart(act)
                    act.activation(G[:, ds(half_ * GB, GB), 4 * j + k, :],
                                   g_bank(t, k)[:, 0:GB * NK].rearrange("p (b n) -> p b n", b=GB),
                                   ACT.Copy).then_inc(s["a_G"], 1)

                def pt_high(c):
                    wait(act, "s_PT", 4 * t + c + 1)
                    if c == 0:
                        wait(act, "s_O", 3 * (t - 1))
                        if at_slot(t, 0, 1):
                            act.wait_ge(s["pt_zero"], 2)
                    act.activation(pt_hi[0:NK, j % 2, c * 512:(c + 1) * 512], QB[q_bank(j, c)][0:NK, :],
                                   ACT.Copy).then_inc(s["a_PThi"], 1)

                def oT(k):
                    wait(act, "s_out", t - 1)
                    wait(act, "s_T", 2 * (t - 1) + k + 1)
                    bank_ = WB[1 + k][:, :].rearrange("p (c n) -> p c n", c=4)
                    act.activation(OT_hi[:, 4 * k:4 * k + 4, :], bank_, ACT.Copy)
                    act.activation(OT[:, 4 * k:4 * k + 4, :], bank_, ACT.Copy).then_inc(s["a_T"], 1)

                now, gon, old = on(t, 0, NB), on(t, FIRST, NB - GB), on(t, 1, NB + 1)
                if now:
                    v_high(0); v_high(1); exps(0); exps(1)
                if gon:
                    g_out(0)
                if now:
                    exps(2)
                if now:
                    pt_high(0)
                if gon:
                    g_out(1)
                if now:
                    pt_high(1)
                if gon:
                    g_out(2)
                if on(t, -1, NB - 1):
                    wait(act, "s_xT", t + 2)
                    wait(act, "s_S", 3 * t)
                    act.activation(xT[:, (j + 1) % 2, :], QB[x_bank(j)][:, 0:NQ], ACT.Copy).then_inc(s["a_xT"], 1)
                if gon:
                    g_out(3)
                if on(t + 1, FIRST, NB - GB) and j == GB - 1:
                    context_high(t + 1)
                if now:
                    pt_high(2); pt_high(3)
                if old:
                    oT(0); oT(1)
                if at_slot(t, HEAD + 2):
                    x2_high(0)
                if at_slot(t, HEAD + 4):
                    act.wait_ge(s["ld_w2"], 16)
                    act.wait_ge(s["s_S"], 3 * NB)
                    act.activation(w2_hi[:, :], w2_raw, ACT.Copy).then_inc(s["w2_hi_done"], 1)
                if at_slot(t, 0, 1):
                    w, hi, raw = (("w1", w1_hi, w1_raw), ("w3", w3_hi, w3_raw))[t]
                    act.wait_ge(s["ld_" + w], 16)
                    act.activation(hi[:, :], raw, ACT.Copy).then_inc(s[w + "_hi_done"], 1)
                if at_slot(t, FIRST + 2):
                    act.wait_ge(s["scale_step"], 7)
                    act.wait_ge(s["ld_wv"], 16)
                    act.activation(wv_hi[:, :], wv_raw, ACT.Copy, scale=sc[0:DC, 4:5]).then_inc(s["wv_hi_done"], 1)
                if at_slot(t, 1):
                    act.wait_ge(s["wo_step"], 4)
                    act.activation(wo_hi[:, :, :], wo_raw.rearrange("p (c n) -> p c n", c=8), ACT.Copy,
                                   scale=so[:, 3:4]).then_inc(s["wo_hi_done"], 1)
            slots(act, slot)

            def chunk(g, c):
                wait(act, "v_gated", FC * g + max(c - 1, 0))
                act.wait_ge(s["b_a"], FC * g + c + 1)
                act.activation(silu[:, c % 2, :], up_banks(c)[0][:, :], ACT.Silu).then_inc(s["c_silu"], 1)

            def hid_high(g, c):
                wait(act, "b_y", past(g, c, HP))
                act.wait_ge(s["v_hid"], FC * g + c + 1)
                act.activation(hid_hi[:, buffer(c, HP), :], hid[:, buffer(c, HS), :], ACT.Copy).then_inc(s["c_hid"], 1)

            def result_out(g):
                act.wait_ge(s["b_y"], FC * (g + 1))
                act.activation(y_T, WB[2][:, :], ACT.Copy).then_inc(s["c_yT"], 1)

            def group(g, more):
                for c in range(FC):
                    if c == LAG and (not isinstance(g, int) or g > 0):
                        result_out(g - 1)
                    chunk(g, c)
                    if more and c == 12:
                        gates_out(g + 1)
                    if c > 0:
                        hid_high(g, c - 1)
                    elif not isinstance(g, int) or g > 0:
                        hid_high(g - 1, FC - 1)
                    if more and c == 4:
                        x2_high(g + 1)


            gates_out(0)
            group(0, True)
            with act.Fori(1, NG - 1) as g:
                group(g, True)
            group(NG - 1, False)
            hid_high(NG - 1, FC - 1)
            result_out(NG - 1)

        @block.vector
        def _(dve):
            def context_low(t):
                wait(dve, "a_cg", (t + 8) // GB)
                dve.tensor_tensor(cg_lo[:, :], ctx_raw[:, ds((t + 4) * NK, GB * NK)], cg_hi[:, :].bitcast(F),
                                  ALU.subtract).then_inc(s["d_cg"], 1)

            def largest_of(k):
                dve.wait_ge(s["ld_wv" if k == 3 else f"ld_ctx{k}"], 16)
                data = wv_raw if k == 3 else ctx_raw[:, CP[k][0] * NK:CP[k][1] * NK]
                dve.tensor_reduce(amax[0:DC, k:k + 1], data, AX.X, ALU.max,
                                  apply_absolute_value=True).then_inc(s["amax_done"], 1)

            for q in range(4):
                dve.wait_ge(s["a_hi_done"], q + 1)
                dve.scalar_tensor_tensor(a_lo[0:DC, q * 512:(q + 1) * 512], [*SB, QB[0]][q][0:DC, :], DH ** -0.5,
                                         a_hi[0:DC, q * 512:(q + 1) * 512].bitcast(F), ALU.mult,
                                         ALU.subtract).then_inc(s["a_lo_done"], 1)
                if q == 0:
                    dve.wait_ge(s["amax_zero"], 1)
                    largest_of(0)
                if q == 1:
                    context_low(FIRST)
                if q == 2:
                    largest_of(3)
            def scales():
                largest_of(1)
                largest_of(2)
                dve.wait_ge(s["amax_all"], 1)
                dve.tensor_reduce(sc[:, 0:1], amall[:, 0:3], AX.X, ALU.max).then_inc(s["scale_step"], 1)
                dve.tensor_copy(sc[:, 1:2], amall[:, 3:4]).then_inc(s["scale_step"], 1)
                dve.wait_ge(s["scale_step"], 2)
                dve.tensor_scalar(sc[:, 0:2], sc[:, 0:2], TINY, None, ALU.max).then_inc(s["scale_step"], 1)
                dve.wait_ge(s["scale_step"], 3)
                dve.tensor_scalar(sc[:, 2:4].bitcast(U), sc[:, 0:2].bitcast(U), 0x7F800000, None,
                                  ALU.bitwise_and).then_inc(s["scale_step"], 1)
                dve.wait_ge(s["scale_step"], 4)
                dve.tensor_scalar(sc[:, 5:6], sc[:, 2:3], sc[:, 3:4], 1.0 / VBOOST, ALU.mult, ALU.mult).then_inc(s["scale_step"], 1)
                dve.reciprocal(sc[:, 6:8], sc[:, 2:4]).then_inc(s["scale_step"], 1)
                dve.wait_ge(s["scale_step"], 6)
                dve.tensor_scalar(sc[:, 4:5], sc[:, 6:7], sc[:, 7:8], VBOOST, ALU.mult, ALU.mult).then_inc(s["scale_step"], 1)

            def scale_out():
                dve.wait_ge(s["amax_o_all"], 1)
                dve.tensor_scalar(so[:, 0:1], amax_o[:, 1:2], TINY, None, ALU.max).then_inc(s["wo_step"], 1)
                dve.wait_ge(s["wo_step"], 1)
                dve.tensor_scalar(so[:, 1:2].bitcast(U), so[:, 0:1].bitcast(U), 0x7F800000, None,
                                  ALU.bitwise_and).then_inc(s["wo_step"], 1)
                dve.wait_ge(s["wo_step"], 2)
                dve.reciprocal(so[:, 2:3], so[:, 1:2]).then_inc(s["wo_step"], 1)
                dve.wait_ge(s["wo_step"], 3)
                dve.tensor_scalar(so[:, 3:4], so[:, 2:3], WBOOST, None, ALU.mult).then_inc(s["wo_step"], 1)
                dve.tensor_scalar(so[:, 4:5], so[:, 1:2], sc[:, 5:6], 1.0 / WBOOST, ALU.mult, ALU.mult).then_inc(s["wo_step"], 1)
                dve.wait_ge(s["wo_step"], 5)

            steps = []

            def step(ins, g):
                ins.then_inc(s["v_step"], 1)
                steps.append(1)
                dve.wait_ge(s["v_step"], g * STEPS + len(steps))

            STEPS = 15

            def moments(g):
                for i in range(GB):
                    dve.bn_stats(small[:, 16 + 6 * i:22 + 6 * i],
                                 X[:, ds(g * GB + i, 1), :].rearrange("p a n -> p (a n)")).then_inc(s["v_bn"], 1)
                dve.wait_ge(s["v_bn"], GB * (g + 1))
                apart(dve)
                for i in range(GB):
                    last = dve.bn_aggr(small[:, 2 * i:2 * i + 2], small[:, 16 + 6 * i:22 + 6 * i])
                last.then_inc(s["v_aggr"], 1)

            def norm(g):
                wait(dve, "b_x2T", g)
                dve.wait_ge(s["v_aggr"], g + 1)
                dve.wait_ge(s["q_rstd"], g + 1)
                for i in range(GB):
                    last = dve.tensor_scalar(x2[:, i:i + 1, :], X[:, ds(g * GB + i, 1), :], small[:, 2 * i:2 * i + 1],
                                             small[:, 8 + i:9 + i], ALU.subtract, ALU.mult)
                last.then_inc(s["v_x2"], 1)

            at = [64 + 32 * i for i in range(8)]
            tile = lambda n: small[:, at[n]:at[n] + GB * E].rearrange("p (b e) -> p b e", e=E)
            lg, eq, pick, pick2, rest, part = (tile(n) for n in range(6))
            bf, bf2 = (small[:, at[n]:at[n] + GB * E // 2].bitcast(BF).rearrange("p (b e) -> p b e", e=E) for n in (6, 7))
            best, best_rank = small[:, 48:48 + GB], small[:, 52:52 + GB]
            hi, mid, lo = (gate_rows[:, :, GR * n:GR * n + E] for n in range(3))

            def wide(tiles):
                return tiles.unsqueeze(2).broadcast_to([128, GB, E])

            def ties(of, g):
                step(dve.tensor_reduce(best, of, AX.X, ALU.max), g)
                step(dve.tensor_tensor(eq, of, wide(best), ALU.is_equal), g)

            def first(into, g):
                step(dve.tensor_tensor(eq, eq, rank[:, :, :], ALU.mult), g)
                step(dve.tensor_reduce(best_rank, eq, AX.X, ALU.max), g)
                step(dve.tensor_tensor(into, eq, wide(best_rank), ALU.is_equal), g)

            PARTS = 6
            def gates(g, part_):
                if part_ == 0:
                    steps.clear()
                    dve.wait_ge(s["b_lg"], g + 1)
                    step(dve.tensor_copy(lg, misc(g)[:, 0:GB * E].rearrange("p (b e) -> p b e", e=E)), g)
                    ties(lg, g)
                if part_ == 1:
                    first(pick, g)
                if part_ == 2:
                    step(dve.scalar_tensor_tensor(rest, pick, -BIG, lg, ALU.mult, ALU.add), g)
                    ties(rest, g)
                if part_ == 3:
                    first(pick2, g)
                if part_ == 4:
                    step(dve.tensor_tensor(pick, pick, pick2, ALU.add), g)
                    step(dve.tensor_tensor(pick, pick, lg, ALU.mult), g)
                    step(dve.tensor_copy(bf, pick), g)
                    assert len(steps) == STEPS
                if part_ == 5:
                    wait(dve, "b_gT", g)
                    if isinstance(g, int) and g == 0:
                        dve.wait_ge(s["gt_zero"], 2)
                    dve.tensor_tensor(part, pick, bf, ALU.subtract).then_inc(s["v_gate"], 1)
                    dve.tensor_copy(hi, bf).then_inc(s["v_gate"], 1)
                    dve.wait_ge(s["v_gate"], 5 * g + 2)
                    dve.tensor_copy(bf2, part).then_inc(s["v_gate"], 1)
                    dve.wait_ge(s["v_gate"], 5 * g + 3)
                    dve.tensor_tensor(lo, part, bf2, ALU.subtract).then_inc(s["v_gate"], 1)
                    dve.tensor_copy(mid, bf2).then_inc(s["v_gate"], 1)

            def residual(t, j):
                wait(dve, "s_out", t - 1)
                wait(dve, "p_xb", t - 1)
                dve.scalar_tensor_tensor(X[:, ds(t - 2, 1), :], WB[2][:, 0:D].rearrange("p (a n) -> p a n", a=1),
                                         so[:, 4:5], xb[:, j % 2:j % 2 + 1, :], ALU.mult,
                                         ALU.add).then_inc(s["d_res"], 1)

            def slot(t, j):
                def piece_max(p):
                    lo, hi = SP[p]
                    wait(dve, "s_S", 3 * t + p + 1)
                    dve.tensor_reduce(top[:, j % 2, lo:hi], SB[p][:, 0:(hi - lo) * NK].rearrange("p (h k) -> p h k", k=NK),
                                      AX.X, ALU.max).then_inc(s["d_max"], 1)

                def piece_sub(p):
                    lo, hi = SP[p]
                    wait(dve, "d_max", 3 * t + p + 1)
                    if p == 0:
                        wait(dve, "s_PT", 4 * (t - 1))
                        if at_slot(t, 0, 1):
                            dve.wait_ge(s["wv_lo_done"], 1)
                    dve.tensor_tensor(P[:, j % 2, lo * NK:hi * NK].rearrange("p (h k) -> p h k", k=NK),
                                      SB[p][:, 0:(hi - lo) * NK].rearrange("p (h k) -> p h k", k=NK),
                                      top[:, j % 2, lo:hi].unsqueeze(2).broadcast_to([128, hi - lo, NK]),
                                      ALU.subtract).then_inc(s["d_sub"], 1)

                def v_low(k):
                    wait(dve, "a_Vhi", 2 * t + k + 1)
                    dve.tensor_tensor(v_lo[0:NK, j % 2, 8 * k:8 * k + 8, 0:DH],
                                      WB[k][0:NK, :].rearrange("p (h n) -> p h n", h=8),
                                      v_hi[0:NK, j % 2, 8 * k:8 * k + 8, 0:DH], ALU.subtract).then_inc(s["d_Vlo"], 1)

                def piece(p):
                    lo, hi = OP[p]
                    return SB[p][:, 0:(hi - lo) * (DH + 1)].rearrange("p (h n) -> p h n", n=DH + 1)

                def sums(p):
                    lo, hi = OP[p]
                    wait(dve, "s_O", 3 * (t - 1) + p + 1)
                    dve.reciprocal(rec[:, (j + 1) % 2, lo:hi].unsqueeze(2), piece(p)[:, :, DH:DH + 1]).then_inc(s["d_rec"], 1)

                def normed(p):
                    lo, hi = OP[p]
                    wait(dve, "d_rec", 3 * (t - 1) + p + 1)
                    wait(dve, "s_T", 2 * (t - 2))
                    dve.tensor_tensor(O[:, (j + 1) % 2, lo * DH:hi * DH].rearrange("p (h n) -> p h n", n=DH),
                                      piece(p)[:, :, 0:DH],
                                      rec[:, (j + 1) % 2, lo:hi].unsqueeze(2).broadcast_to([128, hi - lo, DH]),
                                      ALU.mult).then_inc(s["d_On"], 1)

                def pt_low(c):
                    wait(dve, "a_PThi", 4 * t + c + 1)
                    dve.tensor_tensor(pt_lo[0:NK, j % 2, c * 512:(c + 1) * 512], QB[q_bank(j, c)][0:NK, :],
                                      pt_hi[0:NK, j % 2, c * 512:(c + 1) * 512], ALU.subtract).then_inc(s["d_PTlo"], 1)

                if on(t, 0, NB):
                    piece_max(0); piece_max(1); piece_sub(0); piece_max(2); piece_sub(1); piece_sub(2)
                if at_slot(t, 2):
                    dve.wait_ge(s["wo_hi_done"], 1)
                    dve.scalar_tensor_tensor(wo_lo[:, :, :], wo_raw.rearrange("p (c n) -> p c n", c=8), so[:, 3:4],
                                             wo_hi[:, :, :], ALU.mult, ALU.subtract).then_inc(s["wo_lo_done"], 1)
                if on(t, -1, NB - 1):
                    wait(dve, "p_rstd", t + 2)
                    wait(dve, "s_xT", t)
                    k = (j + 1) % 2
                    dve.tensor_scalar(xln[:, k:k + 1, :], X[:, ds(t + 1, 1), :], mv[:, k, 0:1], rstd[:, k:k + 1],
                                      ALU.subtract, ALU.mult).then_inc(s["d_xln"], 1)
                if on(t, 0, NB):
                    v_low(0); v_low(1)
                if at_slot(t, HEAD + 4):
                    dve.wait_ge(s["ld_rank"], 16)
                    for part_ in range(PARTS // 2):
                        gates(0, part_)
                if on(t, 1, NB + 1):
                    sums(0); sums(1); normed(0); sums(2); normed(1); normed(2)
                if on(t, 0, NB):
                    pt_low(0); pt_low(1)
                if on(t, 2, NB + 1):
                    residual(t, j)
                if on(t, -1, NB - 1):
                    wait(dve, "a_cv", t + 2)
                    dve.tensor_tensor(cv_lo[:, (j + 1) % 2, :], ctx_raw[:, ds((t + 1) * NK, NK)],
                                      cv_hi[:, (j + 1) % 2, :].bitcast(F), ALU.subtract).then_inc(s["d_cv"], 1)
                if on(t, -2, NB - 2):
                    if isinstance(t, int):
                        dve.wait_ge(s[("ld_x0", "ld_x1", "ld_x2")[min((t + 2) // GB, 2)]], 16)
                    elif j == 2:
                        dve.wait_ge(s["ld_x2"], 16)
                    dve.bn_stats(bn[:, :], X[:, ds(t + 2, 1), :].rearrange("p a n -> p (a n)")).then_inc(s["d_bn"], 1)
                    dve.wait_ge(s["d_bn"], t + 3)
                    apart(dve)
                    dve.bn_aggr(mv[:, j % 2, :], bn[:, :]).then_inc(s["d_aggr"], 1)
                if on(t + 1, FIRST, NB - GB) and j == GB - 1:
                    context_low(t + 1)
                if at_slot(t, HEAD):
                    dve.memset(gate_rows[:, :, :], 0.0).then_inc(s["gt_zero"], 1)
                    moments(0)
                    dve.wait_ge(s["gt_zero"], 1)
                    dve.memset(gate_rows[:, :, E:E + 1], 1.0).then_inc(s["gt_zero"], 1)
                if at_slot(t, HEAD + 1):
                    norm(0)
                if on(t, 0, NB):
                    pt_low(2); pt_low(3)
                if at_slot(t, HEAD + 4):
                    for part_ in range(PARTS // 2, PARTS):
                        gates(0, part_)
                if at_slot(t, FIRST):
                    scales()
                if at_slot(t, 0):
                    dve.wait_ge(s["ld_wo"], 16)
                    dve.tensor_reduce(amax_o[:, 0:1], wo_raw, AX.X, ALU.max,
                                      apply_absolute_value=True).then_inc(s["amax_o_done"], 1)
                if at_slot(t, 1):
                    scale_out()
                if at_slot(t, FIRST + 3):
                    dve.wait_ge(s["wv_hi_done"], 1)
                    dve.scalar_tensor_tensor(wv_lo[:, :], wv_raw, sc[0:DC, 4:5], wv_hi[:, :].bitcast(F), ALU.mult,
                                             ALU.subtract).then_inc(s["wv_lo_done"], 1)
            slots(dve, slot)

            def chunk(g, c, more):
                wait(dve, "r_hid", past(g, c, HS))
                if c == 0:
                    wait(dve, "v_hid", FC * g)
                dve.wait_ge(s["b_g"], FC * g + c + 1)
                dve.wait_ge(s["c_silu"], FC * g + c + 1)
                dve.tensor_tensor(gated[:, c % 2, :], WB[c % 2][:, :], silu[:, c % 2, :], ALU.mult).then_inc(s["v_gated"], 1)
                if more and c >= FC - 1 - PARTS and c < FC - 1:
                    gates(g + 1, c - (FC - 1 - PARTS))
                if c < FC - 1:
                    dve.wait_ge(s["b_b"], (FC - 1) * g + c + 1)
                dve.wait_ge(s["v_gated"], FC * g + c + 1)
                if c < FC - 1:
                    out, up, gate = hid[:, buffer(c, HS), :], up_banks(c)[1][:, :], gated[:, c % 2, :]
                else:
                    out, up, gate = hid[0:64, HS, :], up_banks(c)[1][64:128, :], gated[0:64, c % 2, :]
                dve.tensor_tensor(out, up, gate, ALU.mult).then_inc(s["v_hid"], 1)

            def group(g, more):
                for c in range(FC):
                    chunk(g, c, more)
                    if isinstance(g, int) and g == 0 and c == 1:
                        residual(LAST, LAST % GB)
                    if more and c == 0:
                        moments(g + 1)
                    if more and c == 2:
                        norm(g + 1)
                    if c == LAG and (not isinstance(g, int) or g > 0):
                        result(g - 1)

            def result(g):
                dve.wait_ge(s["b_yt"], g + 1)
                dve.tensor_tensor(X[:, ds(g * GB, GB), :], QB[1][:, :].rearrange("p (b n) -> p b n", b=GB),
                                  X[:, ds(g * GB, GB), :], ALU.add).then_inc(s["v_out"], 1)

            dve.wait_ge(s["w2_hi_done"], 1)
            dve.wait_ge(s["s_O"], 3 * NB)
            dve.tensor_tensor(w2_lo[:, :], w2_raw, w2_hi[:, :].bitcast(F), ALU.subtract).then_inc(s["w2_lo_done"], 1)
            dve.wait_ge(s["w2_lo_done"], 1)
            dve.memset(hid[64:128, HS, :], 0.0)
            group(0, True)
            with dve.Fori(1, NG - 1) as g:
                group(g, True)
            group(NG - 1, False)
            result(NG - 1)

        @block.tensor
        def _(pe):
            for q in range(4):
                pe.wait_ge(s["ld_qk0" if q == 0 else "ld_qk1"], 32)
                for i in range(4):
                    h = 4 * q + i
                    last = pe.matmul([*SB, QB[0]][q][0:DC, i * D:(i + 1) * D], wk_raw[:, h * DC:(h + 1) * DC],
                                     wq_raw[:, h * D:(h + 1) * D], start=True, stop=True)
                last.then_inc(s["a_mm"], 1)

            def three(out, w_hi, w_lo, m_hi, m_lo):
                pe.matmul(out, w_hi, m_hi, start=True, stop=False)
                pe.matmul(out, w_hi, m_lo, start=False, stop=False)
                return pe.matmul(out, w_lo, m_hi, start=False, stop=True)

            def x2_turn(g):
                pe.wait_ge(s["v_x2"], g + 1)
                wait(pe, "v_out", g - 1)
                for i in range(GB):
                    last = pe.transpose(misc(g)[:, i * NQ:(i + 1) * NQ], x2[:, i, :], ident[:, :])
                last.then_inc(s["b_x2T"], 1)

            def logits(g):
                pe.wait_ge(s["c_x2T"], g + 1)
                for i in range(GB):
                    last = pe.matmul(misc(g)[:, i * E:(i + 1) * E], x2T[:, i * NQ:(i + 1) * NQ], rw[:, :],
                                     start=True, stop=True)
                last.then_inc(s["b_lg"], 1)

            def gates_turn(g):
                pe.wait_ge(s["v_gate"], 5 * g + 5)
                for i in range(GB):
                    last = pe.transpose(misc(g)[:, i * NQ:(i + 1) * NQ], gate_rows[:, i, :], ident[:, :])
                last.then_inc(s["b_gT"], 1)

            def project(t, j):
                if on(t, FIRST, NB - GB):
                    wait(pe, "a_G", 4 * (t + 4) + 1)
                if at_slot(t, 2):
                    pe.wait_ge(s["wo_lo_done"], 1)
                wait(pe, "r_T", 2 * (t - 1))
                for c in range(8):
                    pe.matmul(WB[2][:, 0:D], OT_hi[:, c, :], wo_hi[:, c, :], start=(c == 0), stop=False)
                    pe.matmul(WB[2][:, 0:D], OT_hi[:, c, :], wo_lo[:, c, :], start=False, stop=False)
                    last = pe.matmul(WB[2][:, 0:D], OT_lo[:, c, :], wo_hi[:, c, :], start=False, stop=(c == 7))
                last.then_inc(s["s_out"], 1)

            def slot(t, j):
                def scores():
                    wait(pe, "a_xT", t + 1)
                    wait(pe, "a_G", 4 * (t - j) + 16)
                    half_ = (t // GB) % 2 if isinstance(t, int) else (t // GB) % 2
                    for p, (lo, hi) in enumerate(SP):
                        wait(pe, "d_On", 3 * (t - 2) + p + 1)
                        pe.matmul(SB[p][:, 0:(hi - lo) * NK], xT[:, j % 2, :],
                                  G_flat[:, ds((half_ * GB + j) * HK + lo * NK, (hi - lo) * NK)],
                                  start=True, stop=True).then_inc(s["s_S"], 1)

                def values(k):
                    wait(pe, "d_cv", t + 1)
                    if k == 0 and at_slot(t, HEAD + 3):
                        pe.wait_ge(s["c_x2T"], 1)
                    if k == 0:
                        wait(pe, "a_G", 4 * (t + 4) if on(t, FIRST, NB - GB) else 4 * (NB - GB))
                    else:
                        wait(pe, "a_T", 2 * (t - 2) + 1)
                    if at_slot(t, 0):
                        pe.wait_ge(s["wv_lo_done"], 1)
                        pe.wait_ge(s["a_G"], 16)
                    cols = slice(k * 512, (k + 1) * 512)
                    three(WB[k][0:NK, :], cv_hi[:, j % 2, :], cv_lo[:, j % 2, :], wv_hi[:, cols],
                          wv_lo[:, cols]).then_inc(s["s_V"], 1)

                def g_piece(k):
                    if k == 0:
                        wait(pe, "d_cg", (t + 8) // GB)
                        wait(pe, "a_T", 2 * (t - 2) + 2)
                        wait(pe, "a_G", 4 * (t + 3) + 1)
                        if isinstance(t, int) and t < 0:
                            pe.wait_ge(s["a_lo_done"], t - FIRST + 1)
                    elif k < 3:
                        if on(t, 0, NB):
                            wait(pe, "d_Vlo", 2 * t + k)
                        else:
                            wait(pe, "a_G", 4 * (t + 3) + k + 1)
                    elif isinstance(t, int) and t < 0:
                        pe.wait_ge(s["a_lo_done"], 4)
                        wait(pe, "a_G", 4 * (t + 2))
                    else:
                        wait(pe, "a_G", 4 * (t + 4) + 2)
                    h = 4 * j + k
                    three(g_bank(t, k)[:, 0:GB * NK], a_hi[0:DC, h * D:(h + 1) * D], a_lo[0:DC, h * D:(h + 1) * D],
                          cg_hi[:, :], cg_lo[:, :]).then_inc(s["s_G"], 1)

                def pv(p):
                    lo, hi = OP[p]
                    b = (j + 1) % 2
                    if on(t, 0, NB):
                        wait(pe, "d_sub", 3 * t + p + 1)
                    else:
                        wait(pe, "d_On", 3 * (t - 2) + p + 1)
                    if p == 0:
                        wait(pe, "d_PTlo", 4 * t)
                        wait(pe, "d_Vlo", 2 * t)
                        if at_slot(t, 1):
                            pe.wait_ge(s["ones_set"], 2)
                    for i, h in enumerate(range(lo, hi)):
                        out = SB[p][:, i * (DH + 1):(i + 1) * (DH + 1)]
                        ph, pl = (w[0:KR, b, h * NQ:(h + 1) * NQ] for w in (pt_hi, pt_lo))
                        pe.matmul(out, ph, v_hi[:, b, h, :], start=True, stop=False)
                        pe.matmul(out, ph, v_lo[:, b, h, :], start=False, stop=False)
                        last = pe.matmul(out, pl, v_hi[:, b, h, :], start=False, stop=True)
                    last.then_inc(s["s_O"], 1)

                def p_turn(c):
                    wait(pe, "a_exp", 3 * t + (1, 2, 2, 3)[c])
                    if c < 3:
                        wait(pe, "d_PTlo", 4 * t + (-1, 0, 2)[c])
                    elif on(t, -1, NB - 1):
                        wait(pe, "a_xT", t + 2)
                    else:
                        wait(pe, "d_PTlo", 4 * t + 1)
                    for i in range(4):
                        h = 4 * c + i
                        last = pe.transpose(QB[q_bank(j, c)][0:NK, i * NQ:(i + 1) * NQ],
                                            P[:, j % 2, h * NK:(h + 1) * NK], ident[:, :])
                    last.then_inc(s["s_PT"], 1)

                def o_turn(k):
                    wait(pe, "d_On", 3 * (t - 1) + k + 2)
                    if k == 0:
                        if on(t, FIRST, NB - GB):
                            wait(pe, "a_G", 4 * (t + 4) + 3)
                        elif on(t, 0, NB):
                            wait(pe, "d_Vlo", 2 * t + 2)
                        else:
                            wait(pe, "a_T", 2 * (t - 2) + 1)
                    else:
                        wait(pe, "d_res", t - 1)
                    for i in range(4):
                        c = 4 * k + i
                        last = pe.transpose(WB[1 + k][:, i * NQ:(i + 1) * NQ], O[:, (j + 1) % 2, c * 128:(c + 1) * 128], ident[:, :])
                    last.then_inc(s["s_T"], 1)

                now, gon, old = on(t, 0, NB), on(t, FIRST, NB - GB), on(t, 1, NB + 1)
                if now:
                    scores(); values(0); values(1)
                if gon:
                    g_piece(0)
                if old:
                    pv(0); pv(1); pv(2)
                if now:
                    p_turn(0)
                if gon:
                    g_piece(1)
                if now:
                    p_turn(1)
                if gon:
                    g_piece(2)
                if on(t, 2, NB + 1):
                    project(t, j)
                if on(t, -1, NB - 1):
                    wait(pe, "d_xln", t + 2)
                    if at_slot(t, -1):
                        pe.wait_ge(s["ld_id"], 16)
                    wait(pe, "d_PTlo", 4 * t + 1)
                    pe.transpose(QB[x_bank(j)][:, 0:NQ], xln[:, (j + 1) % 2, :], ident[:, :]).then_inc(s["s_xT"], 1)
                if gon:
                    g_piece(3)
                if now:
                    p_turn(2); p_turn(3)
                if old:
                    o_turn(0); o_turn(1)
                if at_slot(t, HEAD + 3):
                    pe.wait_ge(s["ld_rw"], 16)
                if at_slot(t, HEAD + 2, HEAD + 3):
                    pe.wait_ge(s["d_Vlo"], 2 * t + 1)
                    (x2_turn, logits)[t - HEAD - 2](0)
            slots(pe, slot)

            def up(g, c):
                at, cols = ds(g % 2 * NT, NT), slice(c * 128, (c + 1) * 128)
                before = FC * g + max(c - 1, 0)
                if c == 0:
                    wait(pe, "r_x2lo", g + 1)
                last = c == FC - 1
                if c in (0, 1, 3):
                    wait(pe, "v_hid", FC * g + (-2, 0, None, 1)[c])
                else:
                    wait(pe, "c_silu", before if c != 2 else FC * g + 2)
                three(up_banks(c)[0][:, :], w1_hi[:, cols], w1_lo[:, cols], x2T_hi[:, at], x2T_lo[:, at]).then_inc(s["b_a"], 1)
                if c == 0:
                    if isinstance(g, int) and g == 0:
                        gates_turn(0)
                    pe.wait_ge(s["c_gT"], g + 1)
                wait(pe, "v_gated", before)
                if isinstance(g, int) and g == 0 and c == 1:
                    pe.wait_ge(s["a_T"], 2 * NB)
                pe.matmul(WB[c % 2][:, :], sel[:, cols], gT[:, at], start=True, stop=True).then_inc(s["b_g"], 1)
                if last:
                    return
                if c == 0:
                    wait(pe, "c_silu", FC * g - 1)
                else:
                    wait(pe, "v_hid", before)
                three(up_banks(c)[1][:, :], w3_hi[:, cols], w3_lo[:, cols], x2T_hi[:, at], x2T_lo[:, at]).then_inc(s["b_b"], 1)

            def down(g, c):
                if c == 0:
                    wait(pe, "c_yT", g)
                    if isinstance(g, int) and g == 0:
                        pe.wait_ge(s["w2_lo_done"], 1)
                        pe.wait_ge(s["d_res"], NB)
                pe.wait_ge(s["r_hid"], FC * g + c + 1)
                k, cols, first, final = buffer(c, HP), slice(c * 128, (c + 1) * 128), c == 0, c == FC - 1
                pe.matmul(WB[2][:, :], w2_hi[:, cols], hid_hi[:, k, :], start=first, stop=False)
                pe.matmul(WB[2][:, :], w2_hi[:, cols], hid_lo[:, k, :], start=False, stop=False)
                pe.matmul(WB[2][:, :], w2_lo[:, cols], hid_hi[:, k, :], start=False, stop=final).then_inc(s["b_y"], 1)

            def result_turn(g):
                pe.wait_ge(s["c_yT"], g + 1)
                for i in range(GB):
                    last = pe.transpose(QB[1][:, i * NQ:(i + 1) * NQ], y_T[:, i * D:(i + 1) * D], ident[:, :])
                last.then_inc(s["b_yt"], 1)

            def group(g, more):
                for c in range(FC):
                    up(g, c)
                    if isinstance(g, int) and g == 0 and c == 1:
                        project(LAST, LAST % GB)
                    if more and c == 12:
                        gates_turn(g + 1)
                    if c >= LAG:
                        down(g, c - LAG)
                    elif not isinstance(g, int) or g > 0:
                        down(g - 1, FC - LAG + c)
                    if c == LAG and (not isinstance(g, int) or g > 0):
                        result_turn(g - 1)
                    if more and c == 4:
                        x2_turn(g + 1)
                    if more and c == 5:
                        logits(g + 1)


            pe.wait_ge(s["w_lo_done"], 2)
            pe.wait_ge(s["ld_sel"], 16)
            pe.wait_ge(s["d_PTlo"], 4 * NB)
            pe.wait_ge(s["d_On"], 3 * NB)
            group(0, True)
            with pe.Fori(1, NG - 1) as g:
                group(g, True)
            group(NG - 1, False)
            for c in range(FC - LAG, FC):
                down(NG - 1, c)
            result_turn(NG - 1)


def kernel(x, ctx_768, L0_xattn_w_q, L0_xattn_w_kv, L0_xattn_w_out, L0_xattn_b_out, L0_ffn_router_w,
           L0_ffn_w1, L0_ffn_w2, L0_ffn_w3, L0_ffn_sw1, L0_ffn_sw2, L0_ffn_sw3):
    import concourse.bacc as bacc
    from concourse.bass_utils import run_bass_kernel_spmd

    f = np.float32
    x, ctx = np.asarray(x), np.asarray(ctx_768)
    wq, wkv, wout, bout = (np.asarray(a) for a in (L0_xattn_w_q, L0_xattn_w_kv, L0_xattn_w_out, L0_xattn_b_out))
    w1, w2, w3 = (np.asarray(a) for a in (L0_ffn_w1, L0_ffn_w2, L0_ffn_w3))
    sw1, sw2, sw3 = (np.asarray(a) for a in (L0_ffn_sw1, L0_ffn_sw2, L0_ffn_sw3))
    inner = H * DH
    pad = np.zeros((FP - FU, D), f)
    gap, cut = np.zeros((64 - FL, D), f), (FC - 1) * 128
    first, second = np.concatenate([w1.reshape(E * I, D), sw1]), np.concatenate([w3.reshape(E * I, D), sw3])
    sel = np.zeros((128, FP), f)
    for part in range(3):
        for e in range(E + 1):
            if e < E or part == 0:
                sel[part * GR + e, e * I:(e + 1) * I] = 1.0
    rank = np.broadcast_to(np.arange(E, 0, -1, dtype=f), (128, GB, E))
    arrays = {
        "x": x.transpose(1, 0, 2),
        "ctxT": ctx.transpose(2, 0, 1).reshape(DC, NB * NK),
        "wqT": wq.reshape(D, H, DH).transpose(2, 1, 0).reshape(DH, H * D),
        "wkT": wkv[:, :inner].reshape(DC, H, DH).transpose(2, 1, 0).reshape(DH, H * DC),
        "wv": wkv[:, inner:],
        "wo": wout.reshape(8, 128, D).transpose(1, 0, 2).reshape(128, 8 * D),
        "bo": np.broadcast_to(bout, (128, D)),
        "rwT": np.asarray(L0_ffn_router_w).T,
        "w1T": np.concatenate([first, gap, second[cut:], gap]).T,
        "w3T": second[:cut].T,
        "w2": np.concatenate([w2.transpose(0, 2, 1).reshape(E * I, D), sw2.T, pad]).reshape(FC, 128, D).transpose(1, 0, 2),
        "sel": sel, "ident": np.eye(128, dtype=f), "rank": rank,
    }
    arrays = {n: np.ascontiguousarray(a) for n, a in arrays.items()}
    nc = bacc.Bacc("TRN2", target_bir_lowering=False, num_devices=1)
    ins = [nc.dram_tensor(n + "_in", a.shape, mybir.dt.from_np(a.dtype), kind="ExternalInput").ap() for n, a in arrays.items()]
    out = nc.dram_tensor("y_out", (128, NB, D), mybir.dt.float32, kind="ExternalOutput").ap()
    program(nc, *ins, out)
    got = run_bass_kernel_spmd(nc, [{n + "_in": a for n, a in arrays.items()}], core_ids=[0])
    return got.results[0]["y_out"].transpose(1, 0, 2)
```
